# Optimizing a Trainium2 kernel written in Bass

```python
import numpy as np
import jax
import jax.numpy as jnp

def _softmax(x, axis=-1):
    return jax.nn.softmax(x, axis=axis)

def _gelu(x):
    return jax.nn.gelu(x, approximate=True)

def _silu(x):
    return jax.nn.silu(x)

def _sigmoid(x):
    return jax.nn.sigmoid(x)

def _layernorm(x, axis=-1, eps=1e-05):
    m = jnp.mean(x, axis=axis, keepdims=True)
    v = jnp.var(x, axis=axis, keepdims=True)
    return (x - m) / jnp.sqrt(v + eps)

def _scatter_add(tgt, idx, src, axis=0):
    return tgt.at[idx].add(src)

def _segment_sum(src, seg, n):
    return jax.ops.segment_sum(src, seg, n)
kernel_name = 'mk_decoder_postln_d1_seqx_r8_08af9e'

def setup_inputs(seed: int=0):
    np.random.seed(seed)
    _w = jnp.asarray

    def _rec_inputs():
        import jax
        import jax.numpy as jnp
        _rk = jax.random.key(seed)
        x = -0.0005207 + 1.001 * jax.random.normal(jax.random.fold_in(_rk, 1), (2, 256, 512), jnp.float32)
        _lenS = 256 - jax.random.randint(jax.random.fold_in(_rk, 7), (2,), 0, max(1, 256 // 4) + 1, jnp.int32)
        _lenS2 = 512 - jax.random.randint(jax.random.fold_in(_rk, 8), (2,), 0, max(1, 512 // 4) + 1, jnp.int32)
        _ctx_4096P = jax.random.normal(jax.random.fold_in(_rk, 11), (2, 16, 512), jnp.float32)
        _ctx_4096c = jax.random.dirichlet(jax.random.fold_in(_rk, 511), 0.3 * jnp.ones((16,), jnp.float32), (2, 512))
        _ctx_4096t = jnp.einsum('bsk,bkd->bsd', _ctx_4096c, _ctx_4096P)
        _ctx_4096t = _ctx_4096t * jax.lax.rsqrt(jnp.mean(jnp.square(_ctx_4096t)) + 1e-12) * 0.953939
        ctx_4096 = -0.00010331 + 0.999899 * (_ctx_4096t + 0.3 * jax.random.normal(jax.random.fold_in(_rk, 611), (2, 512, 512), jnp.float32))
        return (x, ctx_4096)
    x, ctx_4096 = _rec_inputs()

    def _L0_attn_setup():
        import jax, jax.numpy as jnp
        import numpy as np
        import math
        D_MODEL = 256
        D_STATE = 16
        EXPAND = 2
        D_INNER = D_MODEL * EXPAND
        DT_RANK = math.ceil(D_MODEL / 16)
        BATCH, SEQ_LEN = (2, 64)
        key = jax.random.key(seed)
        ks = jax.random.split(key, 6)
        x = jax.random.normal(ks[0], (BATCH, SEQ_LEN, D_INNER), dtype=jnp.float32)
        A_log = jnp.log(jax.random.uniform(ks[1], (D_INNER, D_STATE), minval=0.5, maxval=16.0, dtype=jnp.float32))
        D = jnp.ones((D_INNER,), dtype=jnp.float32)
        x_proj_w = 0.02 * jax.random.normal(ks[2], (DT_RANK + 2 * D_STATE, D_INNER), dtype=jnp.float32)
        dt_init_std = DT_RANK ** (-0.5)
        dt_proj_w = jax.random.uniform(ks[3], (D_INNER, DT_RANK), minval=-dt_init_std, maxval=dt_init_std, dtype=jnp.float32)
        dt = jnp.exp(jax.random.uniform(ks[4], (D_INNER,), dtype=jnp.float32) * (math.log(0.1) - math.log(0.001)) + math.log(0.001))
        dt = jnp.clip(dt, 0.0001, None)
        dt_proj_b = dt + jnp.log(-jnp.expm1(-dt))
        return {'x': x, 'A_log': A_log, 'D': D, 'x_proj_w': x_proj_w, 'dt_proj_w': dt_proj_w, 'dt_proj_b': dt_proj_b}
    _L0_attn_all = _L0_attn_setup()
    _L0_attn_in = {k: v for k, v in _L0_attn_all.items() if k in ('A_log', 'D', 'x_proj_w', 'dt_proj_w', 'dt_proj_b')}
    del _L0_attn_all

    def _L0_xattn_setup():
        import jax, jax.numpy as jnp
        import numpy as np
        HEADS = 32
        KV_HEADS = 8
        HEAD_DIM = 128
        EPS = 1e-06

        def rms_norm(x, w):
            var = jnp.mean(jnp.square(x.astype(jnp.float32)), axis=-1, keepdims=True)
            return (x.astype(jnp.float32) * jax.lax.rsqrt(var + EPS)).astype(x.dtype) * w
        key = jax.random.key(seed)
        ks = jax.random.split(key, 6)
        bsz, n_lat, seq, hidden = (8, 64, 512, 512)
        return {'latents': jax.random.normal(ks[0], (bsz, n_lat, hidden), jnp.float32), 'context': jax.random.normal(ks[1], (bsz, seq, hidden), jnp.float32), 'Wq': jax.random.normal(ks[2], (hidden, HEADS * HEAD_DIM), jnp.float32) * 0.02, 'Wk': jax.random.normal(ks[3], (hidden, KV_HEADS * HEAD_DIM), jnp.float32) * 0.02, 'Wv': jax.random.normal(ks[4], (hidden, KV_HEADS * HEAD_DIM), jnp.float32) * 0.02, 'Wo': jax.random.normal(ks[5], (HEADS * HEAD_DIM, hidden), jnp.float32) * 0.02, 'q_norm_w': jnp.ones((HEAD_DIM,), jnp.float32), 'k_norm_w': jnp.ones((HEAD_DIM,), jnp.float32)}
    _L0_xattn_all = _L0_xattn_setup()
    _L0_xattn_in = {k: v for k, v in _L0_xattn_all.items() if k in ('Wq', 'Wk', 'Wv', 'Wo', 'q_norm_w', 'k_norm_w')}
    del _L0_xattn_all

    def _L0_ffn_setup():
        import jax, jax.numpy as jnp
        import numpy as np
        TOP_K = 2
        key = jax.random.key(seed)
        k0, k1, k2 = jax.random.split(key, 3)
        B, S, D, H, E = (4, 256, 512, 512, 8)
        sc = 1.0 / np.sqrt(D).astype(np.float32)
        x = jax.random.normal(k0, (B, S, D), dtype=jnp.float32)
        W_gate = jax.random.normal(k1, (D, E), dtype=jnp.float32) * sc
        b_gate = jnp.zeros((E,), dtype=jnp.float32)
        W_e = jax.random.normal(k2, (E, D, H), dtype=jnp.float32) * sc
        b_e = jnp.zeros((E, H), dtype=jnp.float32)
        return {'x': x, 'W_gate': W_gate, 'b_gate': b_gate, 'W_e': W_e, 'b_e': b_e}
    _L0_ffn_all = _L0_ffn_setup()
    _L0_ffn_in = {k: v for k, v in _L0_ffn_all.items() if k in ('W_gate', 'b_gate', 'W_e', 'b_e')}
    del _L0_ffn_all
    return {'x': x, 'ctx_4096': ctx_4096, 'L0_attn_A_log': _L0_attn_in['A_log'], 'L0_attn_D': _L0_attn_in['D'], 'L0_attn_x_proj_w': _L0_attn_in['x_proj_w'], 'L0_attn_dt_proj_w': _L0_attn_in['dt_proj_w'], 'L0_attn_dt_proj_b': _L0_attn_in['dt_proj_b'], 'L0_xattn_Wq': _L0_xattn_in['Wq'], 'L0_xattn_Wk': _L0_xattn_in['Wk'], 'L0_xattn_Wv': _L0_xattn_in['Wv'], 'L0_xattn_Wo': _L0_xattn_in['Wo'], 'L0_xattn_q_norm_w': _L0_xattn_in['q_norm_w'], 'L0_xattn_k_norm_w': _L0_xattn_in['k_norm_w'], 'L0_ffn_W_gate': _L0_ffn_in['W_gate'], 'L0_ffn_b_gate': _L0_ffn_in['b_gate'], 'L0_ffn_W_e': _L0_ffn_in['W_e'], 'L0_ffn_b_e': _L0_ffn_in['b_e']}

def reference(x, ctx_4096, L0_attn_A_log, L0_attn_D, L0_attn_x_proj_w, L0_attn_dt_proj_w, L0_attn_dt_proj_b, L0_xattn_Wq, L0_xattn_Wk, L0_xattn_Wv, L0_xattn_Wo, L0_xattn_q_norm_w, L0_xattn_k_norm_w, L0_ffn_W_gate, L0_ffn_b_gate, L0_ffn_W_e, L0_ffn_b_e):
    import jax
    import jax.numpy as jnp

    def _L0_attn_ref(x, A_log, D, x_proj_w, dt_proj_w, dt_proj_b):
        import jax, jax.numpy as jnp
        import numpy as np
        import math
        D_MODEL = 256
        D_STATE = 16
        EXPAND = 2
        D_INNER = D_MODEL * EXPAND
        DT_RANK = math.ceil(D_MODEL / 16)
        BATCH, SEQ_LEN = (2, 64)
        A = -jnp.exp(A_log)
        xp = jnp.einsum('bld,rd->blr', x, x_proj_w)
        dt_in = xp[..., :DT_RANK]
        B = xp[..., DT_RANK:DT_RANK + D_STATE]
        C = xp[..., DT_RANK + D_STATE:]
        dt = jax.nn.softplus(jnp.einsum('blr,dr->bld', dt_in, dt_proj_w) + dt_proj_b)
        dA = jnp.exp(dt[..., None] * A)
        dBx = dt[..., None] * B[:, :, None, :] * x[..., None]

        def step(h, inp):
            dA_t, dBx_t, C_t = inp
            h = dA_t * h + dBx_t
            y = jnp.einsum('bdn,bn->bd', h, C_t)
            return (h, y)
        h0 = jnp.zeros((x.shape[0], D_INNER, D_STATE), dtype=x.dtype)
        _, ys = jax.lax.scan(step, h0, (jnp.moveaxis(dA, 1, 0), jnp.moveaxis(dBx, 1, 0), jnp.moveaxis(C, 1, 0)))
        y = jnp.moveaxis(ys, 0, 1) + D * x
        return y

    def _L0_xattn_ref(latents, context, Wq, Wk, Wv, Wo, q_norm_w, k_norm_w):
        import jax, jax.numpy as jnp
        import numpy as np
        HEADS = 32
        KV_HEADS = 8
        HEAD_DIM = 128
        EPS = 1e-06

        def rms_norm(x, w):
            var = jnp.mean(jnp.square(x.astype(jnp.float32)), axis=-1, keepdims=True)
            return (x.astype(jnp.float32) * jax.lax.rsqrt(var + EPS)).astype(x.dtype) * w
        bsz, q_len, hidden = latents.shape
        kv = jnp.concatenate([context, latents], axis=1)
        kv_len = kv.shape[1]
        groups = HEADS // KV_HEADS
        q = (latents @ Wq).reshape(bsz, q_len, HEADS, HEAD_DIM).transpose(0, 2, 1, 3)
        k = (kv @ Wk).reshape(bsz, kv_len, KV_HEADS, HEAD_DIM).transpose(0, 2, 1, 3)
        v = (kv @ Wv).reshape(bsz, kv_len, KV_HEADS, HEAD_DIM).transpose(0, 2, 1, 3)
        q = rms_norm(q, q_norm_w)
        k = rms_norm(k, k_norm_w)
        qg = q.reshape(bsz, KV_HEADS, groups, q_len, HEAD_DIM)
        scale = 1.0 / np.sqrt(HEAD_DIM)
        scores = jnp.einsum('bhgqd,bhkd->bhgqk', qg, k) * scale
        probs = jax.nn.softmax(scores.astype(jnp.float32), axis=-1).astype(q.dtype)
        out = jnp.einsum('bhgqk,bhkd->bhgqd', probs, v)
        out = out.reshape(bsz, HEADS, q_len, HEAD_DIM).transpose(0, 2, 1, 3)
        out = out.reshape(bsz, q_len, HEADS * HEAD_DIM)
        return out @ Wo

    def _L0_ffn_ref(x, W_gate, b_gate, W_e, b_e):
        import jax, jax.numpy as jnp
        import numpy as np
        TOP_K = 2
        logits = x @ W_gate + b_gate
        _, top_idx = jax.lax.top_k(logits, TOP_K)
        y_all = jax.nn.relu(jnp.einsum('bsd,edh->bseh', x, W_e) + b_e)
        y = jnp.take_along_axis(y_all, top_idx[..., None], axis=2)
        return y.mean(axis=2)
    x = _layernorm(x + _L0_attn_ref(x, L0_attn_A_log, L0_attn_D, L0_attn_x_proj_w, L0_attn_dt_proj_w, L0_attn_dt_proj_b), axis=-1)
    x = _layernorm(x + _L0_xattn_ref(x, ctx_4096, L0_xattn_Wq, L0_xattn_Wk, L0_xattn_Wv, L0_xattn_Wo, L0_xattn_q_norm_w, L0_xattn_k_norm_w), axis=-1)
    x = _layernorm(x + _L0_ffn_ref(x, L0_ffn_W_gate, L0_ffn_b_gate, L0_ffn_W_e, L0_ffn_b_e), axis=-1)
    return x

_drawn_inputs = setup_inputs


def setup_inputs(seed=0):
    import zlib

    import numpy as np

    out = dict(_drawn_inputs(seed))
    spreads = {'L0_attn_D': (1.0, 0.2),
     'L0_xattn_q_norm_w': (1.0, 0.2),
     'L0_xattn_k_norm_w': (1.0, 0.2),
     'L0_ffn_b_gate': (0.0, 0.1),
     'L0_ffn_b_e': (0.0, 0.1)}
    factors = {}
    for name, (base, spread) in spreads.items():
        noise = np.random.default_rng([zlib.crc32(name.encode()), seed]).standard_normal(out[name].shape)
        drawn = base * np.exp(spread * noise) if base else spread * noise
        out[name] = jnp.asarray(drawn.astype(out[name].dtype))
    for name, factor in factors.items():
        out[name] = (out[name] * factor).astype(out[name].dtype)
    return out
```

```python
import concourse.bass as bass
from concourse import mybir
from contextlib import ExitStack

fp32 = mybir.dt.float32
fp16 = mybir.dt.float16
u32 = mybir.dt.uint32
ALU = mybir.AluOpType
ACT = mybir.ActivationFunctionType
AX = mybir.AxisListType

P = 128
NB, SX, SC, DM = 2, 256, 512, 512
NT = NB * SX
TT = NT // P
CT = NB * SC // P
HC = DM // P
NS, DTR = 16, 16
NCH = 4
NPC = NS // NCH
KVH, HD, GRP = 8, 128, 4
KX = SX
KL = SC + SX
KT = KL // P
SLOTS = GRP * TT
NE = 8
RMS_EPS, LN_EPS = 1e-6, 1e-5
PIECES = 8 + CT + 8
PC_K, PC_C, PC_V = 0, 8, 16
SLOT_LD = 4


def decoder_layer(nc, xT, pieces, wx, wdt, dtb, alog, dskip, qnw, knw, wa, wb,
                  wg, bg, be, scratch, out):
    ctx = ExitStack()
    with ctx:
        def sb(name, shape, dt=fp32):
            return ctx.enter_context(nc.sbuf_tensor(name, shape, dt))

        def sem(name):
            return ctx.enter_context(nc.semaphore(name))

        class Arena:
            def __init__(self, name, kbytes):
                self.t, self.at, self.size = sb(name, [P, kbytes * 256]), 0, kbytes * 256

            def view(self, words, dt=fp32):
                v = self.t[:, self.at:self.at + words]
                self.at += words
                assert self.at <= self.size, (self.at, self.size)
                return v if dt == fp32 else v.bitcast(dt)

            def again(self):
                self.at = 0

        kTc = [sb(f"kTc_{s}", [P, KVH, NB * SC], fp16) for s in ("hi", "lo")]
        Vc = [sb(f"Vc_{s}", [P, CT, KVH * HD], fp16) for s in ("hi", "lo")]
        x1 = sb("x1", [P, TT, DM])
        ident = sb("ident", [P, P])
        ones = sb("ones", [P, 1])
        half = sb("half", [P, 8])
        dtb_s = sb("dtb_s", [P, HC])
        dsk_s = sb("dsk_s", [P, HC])
        A_s = sb("A_s", [P, HC * NS])
        qkw = sb("qkw", [P, 1])
        knw_s = sb("knw_s", [P, 1])
        ssk = sb("ssk", [P, 2, 4])
        rk = sb("rk", [P, 2, 4])
        lnst = sb("lnst", [P, TT, 6])
        mv = sb("mv", [P, TT, 2])
        rstd = sb("rstd", [P, TT])
        mx = sb("mx", [P, SLOTS])
        negb = sb("negb", [P, SLOTS])
        lsum = sb("lsum", [P, SLOTS])
        rl = sb("rl", [P, SLOTS])
        ssq = sb("ssq", [P, GRP, TT])
        cq = sb("cq", [P, GRP, TT])
        wg_s = sb("wg_s", [P, HC, NE])
        bg_s = sb("bg_s", [P, NE])
        iot = sb("iot", [P, NE])
        RA = Arena("RA", 48)
        pc = [RA.view(PIECES * 256, fp16).rearrange("p (k n) -> p k n", k=PIECES) for _ in range(2)]
        RA.again()
        q = [RA.view(GRP * NT // 2, fp16).rearrange("p (h n) -> p h n", h=GRP) for _ in range(2)]
        sqq = RA.view(NT)
        pt = [[RA.view(KL // 2, fp16).rearrange("p (k n) -> p k n", k=KT) for _ in range(2)] for _ in range(2)]
        oT = [RA.view(GRP * NT // 2, fp16).rearrange("p (h n) -> p h n", h=GRP) for _ in range(2)]
        be_s = RA.view(NE * DM).rearrange("p (e n) -> p e n", e=NE)
        zb = [RA.view(DM) for _ in range(2)]
        rb = [RA.view(DM) for _ in range(2)]
        RB = Arena("RB", 86)
        Bb = RB.view(NS * SX).rearrange("p (n t) -> p n t", n=NS)
        Cb = RB.view(NS * SX).rearrange("p (n t) -> p n t", n=NS)
        xT_s = RB.view(HC * NT).rearrange("p (c t) -> p c t", c=HC)
        dA = [RB.view(NPC * SX) for _ in range(2)]
        W = [RB.view(NPC * SX) for _ in range(NCH)]
        stg = [RB.view(DM) for _ in range(SLOT_LD)]
        dt_s = RB.view(HC * NT).rearrange("p (c t) -> p c t", c=HC)
        kn = RB.view(DM)
        ksq = RB.view(DM)
        u_s = RB.view(SX)
        yt = RB.view(SX)
        wdt_s, xp_s, wx_s = kn, ksq, yt[:, 0:HC * 48].rearrange("p (c r) -> p c r", c=HC)
        dA_all = RB.t[:, 2 * NS * SX + HC * NT:2 * NS * SX + HC * NT + 2 * NPC * SX]
        W_all = RB.t[:, 2 * NS * SX + HC * NT + 2 * NPC * SX:2 * NS * SX + HC * NT + 2 * NPC * SX + NCH * NPC * SX]
        sp_e = dA_all[:, 0:HC * NT].rearrange("p (c t) -> p c t", c=HC)
        sp_l = W_all[:, 0:HC * NT].rearrange("p (c t) -> p c t", c=HC)
        sp_u = W_all[:, HC * NT:2 * HC * NT].rearrange("p (c t) -> p c t", c=HC)
        RB.again()
        kTx = [RB.view(KVH * NT // 2, fp16).rearrange("p (h n) -> p h n", h=KVH) for _ in range(2)]
        Vx = [RB.view(TT * 512, fp16).rearrange("p (k n) -> p k n", k=TT) for _ in range(2)]
        xh = [RB.view(HC * NT // 2, fp16).rearrange("p (c t) -> p c t", c=HC) for _ in range(2)]
        wA = [RB.view(HC * DM // 2, fp16).rearrange("p (c n) -> p c n", c=HC) for _ in range(2)]
        wA_f = RB.view(HC * DM).rearrange("p (c n) -> p c n", c=HC)
        wB = [RB.view(HC * DM // 2, fp16).rearrange("p (c n) -> p c n", c=HC) for _ in range(2)]
        wB_f = RB.view(HC * DM).rearrange("p (c n) -> p c n", c=HC)
        Pb_at = RB.at
        Pb = [RB.view(KL) for _ in range(4)]
        lgt, top, wsel, wtmp = (RB.view(TT * NE).rearrange("p (t e) -> p t e", t=TT) for _ in range(4))
        tix = RB.view(TT * NE, u32).rearrange("p (t e) -> p t e", t=TT)
        tixf = RB.view(TT * 2).rearrange("p (t e) -> p t e", t=TT)
        x2T = RB.t[:, Pb_at:Pb_at + HC * NT].rearrange("p (c t) -> p c t", c=HC)

        def pb(name, banks):
            return ctx.enter_context(nc.psum_tensor(name, [P, banks * 512], fp32))
        PS = [pb("PS0", 2), pb("PS1", 2)]
        PTT, PO, PG = pb("PTT", 2), pb("PO", 1), pb("PG", 1)
        kvp = [PS[0][:, 0:512], PS[0][:, 512:1024]]
        ktp, yp, rp = PS[1][:, 0:512], PS[1][:, 512:768], PTT[:, 0:256]
        four = [PO[:, :], PG[:, :], PTT[:, 0:512], PTT[:, 512:1024]]
        fbank = [PS[0][:, 0:512], PS[0][:, 512:1024], PS[1][:, 0:512], PS[1][:, 512:1024]]

        S = {n: sem(n) for n in (
            "ld_x", "ld_small", "ld_be", "const_ready", "xp_mm", "xp_sb", "bc_out", "dtl_mm", "sp_abs",
            "sp_exp", "sp_ln", "sp_v", "A_exp", "A_ready", "qkw_ready", "split_v", "split_p", "dt_ready",
            "split_hi_v", "split_hi_p",
            "zero_ready", "u_ready", "dA_ready", "dBx_ready", "h_ready", "g_ready", "y_mm", "y_add", "y_ready",
            "r_tr", "r_ev", "kv_mm", "k_sq", "k_ss", "rk_tmp", "k_r", "k_n", "k_tr", "k_hi", "k_lo", "v_hi", "v_lo",
            "ln_st", "ln_mv", "ln_eps", "ln_rstd", "ln_x", "xT_tr", "xT_hi", "xT_lo", "xT_f",
            "a_ld", "a_hi", "a_split", "b_ld", "b_hi", "b_split",
            "s_mm", "mx_done", "negb_done", "exp_done", "rl_done", "norm_done", "t_done", "pt_hi", "pt_lo", "pv_done",
            "o_hi", "o_lo", "wo_mm", "wo_add", "q_mm", "q_hi", "q_sq", "q_lo", "ss_mm", "ss_read", "cq_done",
            "lg_mm", "lg_b", "lg_top", "lg_ix", "lg_f", "lg_eq", "lg_w", "f_mm", "z_done", "relu_done", "acc_done",
            "o_dma", "pool_waited")}
        pc_ld = [sem(f"pc_ld{k}") for k in range(SLOT_LD)]
        bc_ld = [sem(f"bc_ld{c}") for c in range(NCH)]
        N_SMALL = 10
        block = ctx.enter_context(nc.Block())

        @block.sync
        def _(sp):
            sp.dma_start(xT_s, xT.rearrange("(c p) t -> p c t", p=P)).then_inc(S["ld_x"], 16)
            small = [(wx_s, wx.rearrange("(c p) r -> p c r", p=P)), (wdt_s[0:DTR, :], wdt), (dtb_s[:, :], dtb),
                     (A_s[:, :], alog), (dsk_s[:, :], dskip), (qkw[:, :], qnw), (knw_s[:, :], knw)]
            for dst, src in small:
                sp.dma_start(dst, src).then_inc(S["ld_small"], 16)

            def piece(i, k):
                sp.dma_start(stg[k], pieces[i * SLOT_LD + k, :, :]).then_inc(pc_ld[k], 16)

            def bc(b):
                for c in range(NCH):
                    if b:
                        sp.wait_ge(S["g_ready"], HC * NCH * b - NCH + c + 1)
                    for dst, row in ((Bb, 0), (Cb, NS)):
                        src = scratch[row + c * NPC:row + (c + 1) * NPC, b * SX:(b + 1) * SX]
                        sp.dma_start(dst[:, c * NPC:(c + 1) * NPC, :], src.partition_broadcast(P)).then_inc(bc_ld[c], 16)

            for k in range(SLOT_LD):
                piece(0, k)
            sp.wait_ge(S["xp_sb"], 1)
            sp.dma_start(scratch, xp_s[DTR:DTR + 2 * NS, :]).then_inc(S["bc_out"], 16)
            sp.wait_ge(S["bc_out"], 16)
            bc(0)
            with sp.Fori(1, PIECES // SLOT_LD) as i:
                for k in range(SLOT_LD):
                    sp.wait_ge(S["split_v"] if k < 2 else S["split_p"], 2 * i - 1 + k % 2)
                    piece(i, k)
            sp.dma_start(wg_s[:, :, :], wg.rearrange("(c p) e -> p c e", p=P)).then_inc(S["ld_small"], 16)
            sp.dma_start(bg_s[:, :], bg.partition_broadcast(P)).then_inc(S["ld_small"], 16)
            bc(1)
            sp.wait_ge(S["r_ev"], NB * HC)
            sp.wait_ge(S["y_ready"], NB * HC)
            sp.dma_start(wA_f, wa[0]).then_inc(S["a_ld"], 16)
            sp.dma_start(wB_f, wb[0]).then_inc(S["b_ld"], 16)
            sp.wait_ge(S["kv_mm"], 4 * (CT + TT))
            sp.dma_start(be_s, be.partition_broadcast(P)).then_inc(S["ld_be"], 16)
            with sp.Fori(1, KVH + NE // 2) as i:
                sp.wait_ge(S["a_split"], i)
                sp.dma_start(wA_f, wa[i]).then_inc(S["a_ld"], 16)
                sp.wait_ge(S["b_split"], i)
                sp.dma_start(wB_f, wb[i]).then_inc(S["b_ld"], 16)
            for t in range(TT):
                sp.wait_ge(S["ln_x"], 2 * TT + t + 1)
                sp.dma_start(out[t], x1[:, t, :]).then_inc(S["o_dma"], 16)
            sp.wait_ge(S["o_dma"], 16 * TT)

        @block.gpsimd
        def _(pool):
            pool.memset(ident[:, :], 0.0).then_inc(S["const_ready"], 1)
            pool.wait_ge(S["const_ready"], 1)
            pool.affine_select(out=ident[:, :], in_=ident[:, :], compare_op=ALU.not_equal, fill=1.0, base=0,
                               pattern=[[-1, P]], channel_multiplier=1).then_inc(S["const_ready"], 1)
            pool.memset(ones[:, :], 1.0).then_inc(S["const_ready"], 1)
            pool.memset(half[:, :], -0.5).then_inc(S["const_ready"], 1)
            for e in range(NE):
                pool.memset(iot[:, e:e + 1], float(e)).then_inc(S["const_ready"], 1)

            def waited():
                pool.sem_inc(S["pool_waited"], 1)

            def hi_lo(src, hi, lo, s_hi, n, s_lo):
                pool.tensor_scalar(hi, src, 1.0, 1.0, ALU.mult, ALU.mult).then_inc(s_hi, 1)
                pool.wait_ge(s_hi, n + 1)
                pool.tensor_tensor(lo, src, hi, ALU.subtract).then_inc(s_lo, 1)

            for i in range(PIECES // SLOT_LD):
                for k in (2, 3):
                    pool.wait_ge(pc_ld[k], 16 * i + 16)
                    hi_lo(stg[k], pc[0][:, i * SLOT_LD + k, :], pc[1][:, i * SLOT_LD + k, :],
                          S["split_hi_p"], 2 * i + k - 2, S["split_p"])

            def rk_of(j, blk):
                pool.wait_ge(S["k_ss"], 2 * j + blk + 2)
                waited()
                pool.tensor_scalar(rk[:, blk, :], ssk[:, blk, :], 1.0 / HD, RMS_EPS, ALU.mult, ALU.add)\
                    .then_inc(S["rk_tmp"], 1)
                pool.wait_ge(S["rk_tmp"], 2 * j + blk + 1)
                pool.tensor_tensor(rk[:, blk, :], rk[:, blk, :], half[:, 0:4], ALU.pow).then_inc(S["k_r"], 1)

            for b in range(NB):
                with pool.Fori(0, HC) as i:
                    j = i + HC * b
                    for c in range(NCH):
                        pool.wait_ge(bc_ld[c], 32 * (b + 1))
                        if c == 0:
                            pool.wait_ge(S["u_ready"], j + 1)
                        pool.wait_ge(S["y_mm"], NCH * j + c + 1)
                        ub = u_s.unsqueeze(1).broadcast_to([P, NPC, SX])
                        pool.tensor_tensor(W[c].rearrange("p (n t) -> p n t", n=NPC), Bb[:, c * NPC:(c + 1) * NPC, :],
                                           ub, ALU.mult).then_inc(S["dBx_ready"], 1)
                        if c >= 1 and c < 3:
                            rk_of(j, c - 1)

            def w_piece(s, i, c, free=None):
                if free:
                    pool.wait_ge(*free)
                f, w, ld, h, sp_ = ((wA_f, wA, "a_ld", "a_hi", "a_split"), (wB_f, wB, "b_ld", "b_hi", "b_split"))[s]
                if c == 0:
                    pool.wait_ge(S[ld], 16 * i + 16)
                    waited()
                pool.tensor_scalar(w[0][:, c, :], f[:, c, :], 1.0, 1.0, ALU.mult, ALU.mult).then_inc(S[h], 1)
                pool.wait_ge(S[h], 4 * i + c + 1)
                last = pool.tensor_tensor(w[1][:, c, :], f[:, c, :], w[0][:, c, :], ALU.subtract)
                if c == HC - 1:
                    last.then_inc(S[sp_], 1)

            def ln_rstd(k):
                pool.wait_ge(S["ln_mv"], TT * (k + 1))
                pool.tensor_scalar(rstd[:, :], mv[:, :, 1], LN_EPS, 1.0, ALU.add, ALU.mult).then_inc(S["ln_eps"], 1)
                pool.wait_ge(S["ln_eps"], k + 1)
                pool.tensor_tensor(rstd[:, :], rstd[:, :], half[:, 0:TT], ALU.pow).then_inc(S["ln_rstd"], 1)

            ln_rstd(0)
            pool.wait_ge(S["y_ready"], NB * HC)
            pool.wait_ge(S["r_tr"], NB * HC)
            for c in range(HC):
                w_piece(0, 0, c)
            with pool.Fori(CT, CT + TT) as j:
                for blk in range(2):
                    rk_of(j, blk)

            def cq_of(n):
                h = n[1]
                pool.wait_ge(S["ss_read"], 4 * n[0] + h + 1)
                pool.tensor_tensor(cq[:, h, :], ssq[:, h, :], half[:, 0:TT], ALU.pow).then_inc(S["cq_done"], 1)

            for h in range(GRP - 1):
                cq_of((0, h))

            def slot(g, s, first=False, last=False):
                n = SLOTS * g + s
                if not (first and s == 0):
                    pool.wait_ge(S["rl_done"], n)
                    k = (s - 1) % SLOTS
                    waited()
                    pool.tensor_scalar(Pb[(s - 1) % 4], Pb[(s - 1) % 4], rl[:, k:k + 1], 1.0, ALU.mult, ALU.mult)\
                        .then_inc(S["norm_done"], 1)
                if last:
                    return
                if s == 0:
                    if not first:
                        pool.wait_ge(S["exp_done"], n)
                    cq_of((g, 3))
                if s in (1, 3, 5, 7):
                    w_piece(0, g + 1, s // 2, (S["q_mm"], 4 * g + 4) if s == 1 else None)
                if s in (8, 10, 12, 14):
                    w_piece(1, g, s // 2 - 4, (S["wo_mm"], 4 * g) if s == 8 and not first else None)

            def body(g, first=False, final=False):
                for s in range(SLOTS):
                    slot(g, s, first)
                    if not final and s in (10, 12, 14):
                        cq_of((g + 1, s // 2 - 5))

            body(0, first=True)
            with pool.Fori(1, KVH - 1) as g:
                body(g)
            body(KVH - 1, final=True)
            slot(KVH, 0, last=True)
            ln_rstd(1)
            pool.wait_ge(S["wo_mm"], 4 * KVH)
            for c in range(HC):
                w_piece(1, KVH, c)
            with pool.Fori(1, NE // 2) as k:
                for c in range(HC):
                    w_piece(0, KVH + k, c, (S["f_mm"], 8 * k - 4) if c == 0 else None)
                for c in range(HC):
                    w_piece(1, KVH + k, c, (S["f_mm"], 8 * k) if c == 0 else None)
            ln_rstd(2)

        @block.scalar
        def _(act):
            act.wait_ge(S["xp_mm"], 1)
            act.activation(xp_s[0:48, :], PS[1][0:48, 512:1024], ACT.Copy).then_inc(S["xp_sb"], 1)
            act.wait_ge(S["ld_small"], 16 * 7)
            act.activation(A_s[:, :], A_s[:, :], ACT.Exp).then_inc(S["A_exp"], 1)
            for c in range(HC):
                act.wait_ge(S["dtl_mm"], c + 1)
                act.activation(dt_s[:, c, :], four[c], ACT.Abs, bias=dtb_s[:, c:c + 1]).then_inc(S["sp_abs"], 1)
            act.wait_ge(S["sp_abs"], HC)
            act.activation(sp_e, dt_s, ACT.Exp, scale=-1.0).then_inc(S["sp_exp"], 1)
            act.wait_ge(S["sp_exp"], 1)
            act.activation(sp_l, sp_e, ACT.Ln, bias=1.0).then_inc(S["sp_ln"], 1)
            act.wait_ge(S["dt_ready"], 1)
            act.wait_ge(S["A_ready"], 1)
            act.wait_ge(S["zero_ready"], 2)

            def exps(i, b, c):
                j = i + HC * b
                act.wait_ge(S["h_ready"], NCH * j + c + 1)
                for n in range(NPC):
                    last = act.activation(dA[c % 2][:, n * SX + 1:(n + 1) * SX], dt_s[:, i, b * SX + 1:(b + 1) * SX],
                                          ACT.Exp, scale=A_s[:, bass.ds(i * NS + c * NPC + n, 1)])
                last.then_inc(S["dA_ready"], 1)

            def k_square(j, blk):
                act.wait_ge(S["kv_mm"], 4 * j + blk + 1)
                act.wait_ge(S["k_ss"], 2 * j + blk + 1)
                act.activation(ksq, kvp[blk], ACT.Square).then_inc(S["k_sq"], 1)

            def k_high(j, blk, dst):
                act.wait_ge(S["k_tr"], 2 * j + blk + 2)
                act.activation(dst, ktp.rearrange("p (h t) -> p h t", h=4), ACT.Copy, scale=qkw[:, 0:1])\
                    .then_inc(S["k_hi"], 1)

            def v_high(j, blk, dst):
                act.wait_ge(S["kv_mm"], 4 * j + 2 + blk + 1)
                act.activation(dst, kvp[blk], ACT.Copy).then_inc(S["v_hi"], 1)

            act.wait_ge(S["bc_out"], 16)
            act.wait_ge(S["qkw_ready"], 1)
            for b in range(NB):
                with act.Fori(0, HC) as i:
                    j = i + HC * b
                    kd = [kTc[0][:, 4 * k:4 * k + 4, bass.ts(j, P)] for k in range(2)]
                    vd = [Vc[0][:, j, 512 * k:512 * k + 512] for k in range(2)]
                    exps(i, b, 0)
                    exps(i, b, 1)
                    k_square(j, 0)
                    exps(i, b, 2)
                    k_square(j, 1)
                    exps(i, b, 3)
                    v_high(j, 0, vd[0])
                    k_high(j, 0, kd[0])
                    k_high(j, 1, kd[1])
                    v_high(j, 1, vd[1])
                    act.wait_ge(S["r_tr"], j + 1)
                    act.activation(x1[:, 2 * b:2 * b + 2, bass.ts(i, P)], rp.rearrange("p (t c) -> p t c", t=2),
                                   ACT.Copy).then_inc(S["r_ev"], 1)

            def xT_high(k, wide):
                for c in range(HC):
                    act.wait_ge(S["xT_tr"], HC * k + c + 1)
                    if wide:
                        act.activation(x2T[:, c, :], four[c], ACT.Copy).then_inc(S["xT_f"], 1)
                    act.activation(xh[0][:, c, :], four[c], ACT.Copy).then_inc(S["xT_hi"], 1)

            act.wait_ge(S["y_ready"], NB * HC)
            act.wait_ge(S["dBx_ready"], NB * HC * NCH)
            xT_high(0, False)
            with act.Fori(0, TT) as t:
                j = t + CT
                for blk in range(2):
                    k_square(j, blk)
                for blk in range(2):
                    v_high(j, blk, Vx[0][:, t, 512 * blk:512 * blk + 512])
                    k_high(j, blk, kTx[0][:, 4 * blk:4 * blk + 4, bass.ts(t, P)])

            def q_evac(g, h, first=False):
                n = 4 * g + h
                act.wait_ge(S["q_mm"], n + 1)
                act.activation(q[0][:, h, :], PG[:, :], ACT.Copy).then_inc(S["q_hi"], 1)
                if not (first and h == 0):
                    act.wait_ge(S["ss_mm"], n)
                act.activation(sqq, PG[:, :], ACT.Square).then_inc(S["q_sq"], 1)

            def slot(g, s, first=False, final=False):
                n = SLOTS * g + s
                if not (first and s < 2):
                    act.wait_ge(S["t_done"], n - 1)
                    if not (first and s < 4):
                        act.wait_ge(S["pv_done"], n - 3)
                    act.activation(pt[s % 2][0], PTT[:, 0:KL].rearrange("p (k n) -> p k n", k=KT), ACT.Copy)\
                        .then_inc(S["pt_hi"], 1)
                act.wait_ge(S["negb_done"], n + 1)
                if not (first and s < 4):
                    act.wait_ge(S["t_done"], n - 3)
                h, t = s // 4, s % 4
                act.activation(Pb[s % 4], PS[s % 2][:, 0:KL], ACT.Exp, scale=cq[:, h, t:t + 1],
                               bias=negb[:, s:s + 1], accum_out=lsum[:, s:s + 1]).then_inc(S["exp_done"], 1)
                if s % 4 == 2 and not (first and s == 2):
                    h = (s // 4 - 1) % 4
                    act.wait_ge(S["pv_done"], n - 2)
                    if s > 2 and not first:
                        act.wait_ge(S["wo_mm"], 4 * g)
                    act.activation(oT[0][:, h, :], PO[:, :], ACT.Copy).then_inc(S["o_hi"], 1)
                if not final and s in (9, 11, 13, 15):
                    q_evac(g + 1, (s - 9) // 2)

            act.wait_ge(S["kv_mm"], 4 * (CT + TT))
            for h in range(GRP):
                q_evac(0, h, first=True)
            for s in range(SLOTS):
                slot(0, s, first=True)
            with act.Fori(1, KVH - 1) as g:
                for s in range(SLOTS):
                    slot(g, s)
            for s in range(SLOTS):
                slot(KVH - 1, s, final=True)
            for s in range(3):
                n = SLOTS * KVH + s
                if s < 2:
                    act.wait_ge(S["t_done"], n - 1)
                    act.wait_ge(S["pv_done"], n - 3)
                    act.activation(pt[s % 2][0], PTT[:, 0:KL].rearrange("p (k n) -> p k n", k=KT), ACT.Copy)\
                        .then_inc(S["pt_hi"], 1)
                else:
                    act.wait_ge(S["pv_done"], n - 2)
                    act.activation(oT[0][:, 3, :], PO[:, :], ACT.Copy).then_inc(S["o_hi"], 1)
            xT_high(1, True)

            def relu(ep, u, t, first=False):
                J = 8 * ep + 4 * u + t
                act.wait_ge(S["z_done"], J + 1)
                if not (first and u == 0 and t < 2):
                    act.wait_ge(S["acc_done"], J - 1)
                act.activation(rb[t % 2], zb[t % 2], ACT.Relu, scale=wsel[:, t, bass.ds(2 * ep + u, 1)])\
                    .then_inc(S["relu_done"], 1)

            act.wait_ge(S["lg_w"], 1)
            for u in range(2):
                for t in range(TT):
                    relu(0, u, t, first=True)
            with act.Fori(1, NE // 2) as ep:
                for u in range(2):
                    for t in range(TT):
                        relu(ep, u, t)

        @block.vector
        def _(dve):
            dve.wait_ge(S["ld_small"], 16 * 7)
            dve.tensor_tensor(qkw[:, :], qkw[:, :], knw_s[:, :], ALU.mult).then_inc(S["qkw_ready"], 1)
            dve.wait_ge(S["A_exp"], 1)
            dve.tensor_scalar(A_s[:, :], A_s[:, :], -1.0, None, ALU.mult).then_inc(S["A_ready"], 1)
            v = [0]

            def step(ins):
                v[0] += 1
                ins.then_inc(S["sp_v"], 1)
                dve.wait_ge(S["sp_v"], v[0])
            dve.wait_ge(S["sp_exp"], 1)
            step(dve.tensor_scalar(sp_u, sp_e, 1.0, None, ALU.add))
            step(dve.scalar_tensor_tensor(flat(dt_s), flat(sp_u), -1.0, flat(sp_e), ALU.add, ALU.subtract))
            step(dve.reciprocal(sp_u, sp_u))
            step(dve.tensor_tensor(dt_s, dt_s, sp_u, ALU.mult))
            dve.wait_ge(S["sp_ln"], 1)
            step(dve.tensor_tensor(sp_l, sp_l, dt_s, ALU.subtract))
            for c in range(HC):
                last = dve.tensor_scalar(dt_s[:, c, :], four[c], dtb_s[:, c:c + 1], 0.0, ALU.add, ALU.max)
            step(last)
            dve.tensor_tensor(dt_s, dt_s, sp_l, ALU.add).then_inc(S["dt_ready"], 1)
            dve.wait_ge(S["sp_ln"], 1)
            dve.wait_ge(S["dt_ready"], 1)
            for k in range(2):
                z = dA[k].rearrange("p (n t) -> p n t", n=NPC)[:, :, 0:1]
                dve.memset(z, 0.0).then_inc(S["zero_ready"], 1)
            dve.sem_inc(S["y_mm"], NCH)
            dve.sem_inc(S["h_ready"], 2)

            def split(i, k):
                dve.wait_ge(pc_ld[k], 16 * i + 16)
                dve.tensor_copy(pc[0][:, i * SLOT_LD + k, :], stg[k]).then_inc(S["split_hi_v"], 1)
                dve.wait_ge(S["split_hi_v"], 2 * i + k + 1)
                dve.tensor_tensor(pc[1][:, i * SLOT_LD + k, :], stg[k], pc[0][:, i * SLOT_LD + k, :], ALU.subtract)\
                    .then_inc(S["split_v"], 1)
            with dve.Fori(0, PIECES // SLOT_LD) as i:
                split(i, 0)
                split(i, 1)

            def k_sums(j, blk):
                dve.wait_ge(S["k_sq"], 2 * j + blk + 1)
                dve.tensor_reduce(ssk[:, blk, :], ksq.rearrange("p (h d) -> p h d", h=4), AX.X, ALU.add)\
                    .then_inc(S["k_ss"], 1)

            def k_norm(j, blk, first=False):
                dve.wait_ge(S["k_r"], 2 * j + blk + 1)
                dve.wait_ge(S["k_tr"], 2 * j + blk + 1)
                dve.tensor_tensor(kn.rearrange("p (h d) -> p h d", h=4), kvp[blk].rearrange("p (h d) -> p h d", h=4),
                                  rk[:, blk, :].unsqueeze(2).broadcast_to([P, 4, HD]), ALU.mult).then_inc(S["k_n"], 1)

            def k_low(j, blk, hi, lo):
                dve.wait_ge(S["k_hi"], 2 * j + blk + 1)
                dve.scalar_tensor_tensor(lo, ktp.rearrange("p (h t) -> p h t", h=4), qkw[:, 0:1], hi,
                                         ALU.mult, ALU.subtract).then_inc(S["k_lo"], 1)

            def v_low(j, blk, hi, lo):
                dve.wait_ge(S["v_hi"], 2 * j + blk + 1)
                dve.tensor_tensor(lo, kvp[blk], hi, ALU.subtract).then_inc(S["v_lo"], 1)

            for b in range(NB):
                with dve.Fori(0, HC) as i:
                    j = i + HC * b
                    kd = [[kTc[w][:, 4 * k:4 * k + 4, bass.ts(j, P)] for w in range(2)] for k in range(2)]
                    vd = [[Vc[w][:, j, 512 * k:512 * k + 512] for w in range(2)] for k in range(2)]

                    def scan(c):
                        dve.wait_ge(S["dA_ready"], NCH * j + c + 1)
                        dve.wait_ge(S["dBx_ready"], NCH * j + c + 1)
                        dve.tensor_tensor_scan(W[c], dA[c % 2], W[c], 0.0, ALU.mult, ALU.add).then_inc(S["h_ready"], 1)
                        dve.wait_ge(S["h_ready"], NCH * j + c + 3)
                        dve.tensor_tensor(W[c], W[c], Cb[:, c * NPC:(c + 1) * NPC, :].rearrange("p n t -> p (n t)"),
                                          ALU.mult).then_inc(S["g_ready"], 1)

                    xs = xT_s[:, i, b * SX:(b + 1) * SX]
                    dve.tensor_tensor(u_s, dt_s[:, i, b * SX:(b + 1) * SX], xs, ALU.mult).then_inc(S["u_ready"], 1)
                    scan(0)
                    scan(1)
                    k_sums(j, 0)
                    scan(2)
                    k_sums(j, 1)
                    k_norm(j, 0)
                    scan(3)
                    v_low(j, 0, *vd[0])
                    k_low(j, 0, *kd[0])
                    k_norm(j, 1)
                    dve.wait_ge(S["y_mm"], NCH * j + 2 * NCH)
                    dve.scalar_tensor_tensor(yt, xs, dsk_s[:, bass.ds(i, 1)], yp, ALU.mult, ALU.add)\
                        .then_inc(S["y_add"], 1)
                    dve.wait_ge(S["y_add"], j + 1)
                    dve.tensor_tensor(yt, yt, xs, ALU.add).then_inc(S["y_ready"], 1)
                    k_low(j, 1, *kd[1])
                    v_low(j, 1, *vd[1])

            def norm(k):
                for t in range(TT):
                    dve.bn_stats(lnst[:, t, :], x1[:, t, :]).then_inc(S["ln_st"], 1)
                for t in range(TT):
                    dve.wait_ge(S["ln_st"], TT * k + t + 1)
                    dve.bn_aggr(mv[:, t, :], lnst[:, t, :]).then_inc(S["ln_mv"], 1)
                dve.wait_ge(S["ln_rstd"], k + 1)
                dve.wait_ge(S["ln_mv"], TT * (k + 1))
                for t in range(TT):
                    dve.tensor_scalar(x1[:, t, :], x1[:, t, :], mv[:, t, 0:1], rstd[:, t:t + 1],
                                      ALU.subtract, ALU.mult).then_inc(S["ln_x"], 1)

            def xT_low(k):
                for c in range(HC):
                    dve.wait_ge(S["xT_hi"], HC * k + c + 1)
                    dve.tensor_tensor(xh[1][:, c, :], four[c], xh[0][:, c, :], ALU.subtract).then_inc(S["xT_lo"], 1)

            dve.wait_ge(S["r_ev"], NB * HC)
            norm(0)
            dve.wait_ge(S["dBx_ready"], NB * HC * NCH)
            xT_low(0)
            with dve.Fori(0, TT) as t:
                j = t + CT
                kd = [[kTx[w][:, 4 * k:4 * k + 4, bass.ts(t, P)] for w in range(2)] for k in range(2)]
                k_sums(j, 0)
                k_sums(j, 1)
                k_norm(j, 0)
                k_norm(j, 1)
                for blk in range(2):
                    v_low(j, blk, *[Vx[w][:, t, 512 * blk:512 * blk + 512] for w in range(2)])
                    k_low(j, blk, *kd[blk])

            def q_low(g, h):
                dve.wait_ge(S["q_hi"], 4 * g + h + 1)
                dve.wait_ge(S["q_sq"], 4 * g + h + 1)
                dve.tensor_tensor(q[1][:, h, :], PG[:, :], q[0][:, h, :], ALU.subtract).then_inc(S["q_lo"], 1)

            def ss_evac(g, h):
                dve.wait_ge(S["ss_mm"], 4 * g + h + 1)
                dve.tensor_scalar(ssq[:, h, :], PG[:, 0:TT], HD * RMS_EPS, None, ALU.add).then_inc(S["ss_read"], 1)

            def pt_low(n, s):
                dve.wait_ge(S["pt_hi"], n - 1)
                dve.tensor_tensor(pt[s % 2][1], PTT[:, 0:KL].rearrange("p (k n) -> p k n", k=KT), pt[s % 2][0],
                                  ALU.subtract).then_inc(S["pt_lo"], 1)

            def o_low(n, h):
                dve.wait_ge(S["o_hi"], n)
                dve.tensor_tensor(oT[1][:, h, :], PO[:, :], oT[0][:, h, :], ALU.subtract).then_inc(S["o_lo"], 1)

            def wo_add(g, t):
                dve.wait_ge(S["wo_mm"], 4 * g + t + 1)
                dve.tensor_tensor(x1[:, t, :], x1[:, t, :], PG[:, :], ALU.add).then_inc(S["wo_add"], 1)

            def recip(n, s):
                dve.wait_ge(S["exp_done"], n)
                k = (s - 1) % SLOTS
                dve.reciprocal(rl[:, k:k + 1], lsum[:, k:k + 1]).then_inc(S["rl_done"], 1)

            def slot(g, s, first=False, final=False):
                n = SLOTS * g + s
                if not (first and s == 0):
                    recip(n, s)
                dve.wait_ge(S["s_mm"], n + 1)
                dve.reduce_max(mx[:, s:s + 1], PS[s % 2][:, 0:KL], AX.X).then_inc(S["mx_done"], 1)
                if s % 4 == 0:
                    dve.wait_ge(S["cq_done"], 4 * g + s // 4 + 1)
                dve.wait_ge(S["mx_done"], n + 1)
                dve.scalar_tensor_tensor(negb[:, s:s + 1], mx[:, s:s + 1], -1.0, cq[:, s // 4, s % 4:s % 4 + 1],
                                         ALU.mult, ALU.mult).then_inc(S["negb_done"], 1)
                if not (first and s < 2):
                    pt_low(n, s)
                if s % 4 == 2 and not (first and s == 2):
                    o_low(4 * g + s // 4, (s // 4 - 1) % 4)
                if s == 0:
                    ss_evac(g, 3)
                if s in (3, 4, 5, 6) and not first:
                    wo_add(g - 1, s - 3)
                if not final:
                    if s in (9, 11, 13, 15):
                        q_low(g + 1, (s - 9) // 2)
                    if s in (10, 12, 14):
                        ss_evac(g + 1, (s - 10) // 2)

            dve.wait_ge(S["kv_mm"], 4 * (CT + TT))
            for h in range(GRP):
                q_low(0, h)
                if h < GRP - 1:
                    ss_evac(0, h)
            for s in range(SLOTS):
                slot(0, s, first=True)
            with dve.Fori(1, KVH - 1) as g:
                for s in range(SLOTS):
                    slot(g, s)
            for s in range(SLOTS):
                slot(KVH - 1, s, final=True)
            recip(SLOTS * KVH, 0)
            for s in range(2):
                pt_low(SLOTS * KVH + s, s)
            o_low(4 * KVH, 3)
            for t in range(TT):
                wo_add(KVH - 1, t)
            dve.wait_ge(S["wo_add"], 4 * KVH)
            norm(1)
            xT_low(1)
            dve.wait_ge(S["const_ready"], 4 + NE)
            dve.wait_ge(S["ld_small"], 16 * 9)
            for t in range(TT):
                dve.wait_ge(S["lg_mm"], TT)
                dve.tensor_tensor(lgt[:, t, :], fbank[0][:, t * NE:(t + 1) * NE], bg_s[:, :], ALU.add)\
                    .then_inc(S["lg_b"], 1)
            for t in range(TT):
                dve.wait_ge(S["lg_b"], t + 1)
                dve.max(top[:, t, :], lgt[:, t, :]).then_inc(S["lg_top"], 1)
            for t in range(TT):
                dve.wait_ge(S["lg_top"], t + 1)
                dve.max_index(tix[:, t, :], top[:, t, :], lgt[:, t, :]).then_inc(S["lg_ix"], 1)
            dve.wait_ge(S["lg_ix"], TT)
            dve.tensor_copy(tixf[:, :, :], tix[:, :, 0:2]).then_inc(S["lg_f"], 1)
            dve.wait_ge(S["lg_f"], 1)
            for t in range(TT):
                dve.tensor_scalar(wsel[:, t, :], iot[:, :], tixf[:, t, 0:1], 0.5, ALU.is_equal, ALU.mult)\
                    .then_inc(S["lg_eq"], 1)
                dve.tensor_scalar(wtmp[:, t, :], iot[:, :], tixf[:, t, 1:2], 0.5, ALU.is_equal, ALU.mult)\
                    .then_inc(S["lg_eq"], 1)
            dve.wait_ge(S["lg_eq"], 2 * TT)
            dve.tensor_tensor(wsel[:, :, :], wsel[:, :, :], wtmp[:, :, :], ALU.add).then_inc(S["lg_w"], 1)
            dve.wait_ge(S["ld_be"], 16)

            def bias(ep, u, t, first=False):
                J = 8 * ep + 4 * u + t
                dve.wait_ge(S["f_mm"], J + 1)
                if not (first and u == 0 and t < 2):
                    dve.wait_ge(S["relu_done"], J - 1)
                dve.tensor_tensor(zb[t % 2], fbank[t], be_s[:, 2 * ep + u, :], ALU.add).then_inc(S["z_done"], 1)

            def gather(J, t):
                dve.wait_ge(S["relu_done"], J + 1)
                dve.tensor_tensor(x1[:, t, :], x1[:, t, :], rb[t % 2], ALU.add).then_inc(S["acc_done"], 1)

            for u in range(2):
                for t in range(TT):
                    bias(0, u, t, first=True)
                    if u or t:
                        if 4 * u + t > 4:
                            dve.wait_ge(S["acc_done"], 4 * u + t - 4)
                        gather(4 * u + t - 1, (t - 1) % 4)
            with dve.Fori(1, NE // 2) as ep:
                for u in range(2):
                    for t in range(TT):
                        bias(ep, u, t)
                        J = 8 * ep + 4 * u + t
                        dve.wait_ge(S["acc_done"], J - 4)
                        gather(J - 1, (t - 1) % 4)
            gather(4 * NE - 1, 3)
            dve.wait_ge(S["acc_done"], 4 * NE)
            norm(2)

        @block.tensor
        def _(pe):
            pe.wait_ge(S["ld_x"], 16)
            pe.wait_ge(S["ld_small"], 16 * 7)
            for c in range(HC):
                last = pe.matmul(PS[1][0:48, 512:1024], wx_s[:, c, :], xT_s[:, c, :], start=(c == 0), stop=(c == HC - 1))
            last.then_inc(S["xp_mm"], 1)
            pe.wait_ge(S["xp_sb"], 1)
            for c in range(HC):
                pe.matmul(four[c], wdt_s[0:DTR, c * P:(c + 1) * P], xp_s[0:DTR, :], start=True, stop=True)\
                    .then_inc(S["dtl_mm"], 1)
            pe.wait_ge(S["const_ready"], 2)
            pe.wait_ge(S["dt_ready"], 1)

            PASS = ((0, 0), (0, 1), (1, 0))

            def kv_block(j, blk, src, w0):
                if blk < 2:
                    pe.wait_ge(S["v_lo"], 2 * j + blk + 1)
                else:
                    pe.wait_ge(S["k_n"], 2 * j + blk - 1)
                m = 0
                for a, w in PASS:
                    for c in range(HC):
                        last = pe.matmul(kvp[blk % 2], src(a, c), pc[w][:, w0 + c, :], start=(m == 0), stop=(m == 11))
                        m += 1
                last.then_inc(S["kv_mm"], 1)

            def k_transpose(j, blk):
                pe.wait_ge(S["k_n"], 2 * j + blk + 1)
                pe.wait_ge(S["k_lo"], 2 * j + blk + 1)
                for h in range(4):
                    last = pe.transpose(ktp[:, h * P:(h + 1) * P], kn[:, h * P:(h + 1) * P], ident[:, :])
                last.then_inc(S["k_tr"], 1)

            def y_sum(j, c):
                pe.wait_ge(S["g_ready"], NCH * j + c + 1)
                for n in range(NPC):
                    last = pe.matmul(yp, ident[:, :], W[c][:, n * SX:(n + 1) * SX], start=(c == 0 and n == 0),
                                     stop=(c == NCH - 1 and n == NPC - 1))
                last.then_inc(S["y_mm"], 1)

            pe.sem_inc(S["v_lo"], 2)
            pe.sem_inc(S["k_lo"], 1)
            pe.sem_inc(S["k_tr"], 1)
            pe.sem_inc(S["k_ss"], 1)
            pe.wait_ge(S["split_v"], PIECES // 2)
            pe.wait_ge(S["split_p"], PIECES // 2)
            for b in range(NB):
                with pe.Fori(0, HC) as i:
                    j = i + HC * b

                    def src(a, c):
                        return pc[a][:, PC_C + j, c * P:(c + 1) * P]
                    kv_block(j, 0, src, PC_K)
                    kv_block(j, 1, src, PC_K + 4)
                    y_sum(j, 0)
                    y_sum(j, 1)
                    kv_block(j, 2, src, PC_V)
                    k_transpose(j, 0)
                    y_sum(j, 2)
                    k_transpose(j, 1)
                    y_sum(j, 3)
                    kv_block(j, 3, src, PC_V + 4)
                    pe.wait_ge(S["y_ready"], j + 1)
                    for t in range(2):
                        last = pe.transpose(rp[:, t * P:(t + 1) * P], yt[:, t * P:(t + 1) * P], ident[:, :])
                    last.then_inc(S["r_tr"], 1)

            def xT_transpose(k):
                for c in range(HC):
                    for t in range(TT):
                        if c == 0:
                            pe.wait_ge(S["ln_x"], TT * k + t + 1)
                        last = pe.transpose(four[c][:, t * P:(t + 1) * P], x1[:, t, c * P:(c + 1) * P], ident[:, :])
                    last.then_inc(S["xT_tr"], 1)
            pe.wait_ge(S["r_ev"], NB * HC)
            xT_transpose(0)
            pe.wait_ge(S["xT_lo"], HC)
            with pe.Fori(0, TT) as t:
                j = t + CT

                def srcx(a, c):
                    return xh[a][:, c, bass.ts(t, P)]
                kv_block(j, 0, srcx, PC_K)
                kv_block(j, 1, srcx, PC_K + 4)
                kv_block(j, 2, srcx, PC_V)
                k_transpose(j, 0)
                kv_block(j, 3, srcx, PC_V + 4)
                k_transpose(j, 1)

            def q_job(g, h):
                if h == 0:
                    pe.wait_ge(S["a_split"], g + 1)
                m = 0
                for w, a in PASS:
                    for c in range(HC):
                        last = pe.matmul(PG[:, :], wA[w][:, c, h * HD:(h + 1) * HD], xh[a][:, c, :],
                                         start=(m == 0), stop=(m == 11))
                        m += 1
                last.then_inc(S["q_mm"], 1)

            def ss_job(g, h):
                pe.wait_ge(S["q_sq"], 4 * g + h + 1)
                pe.wait_ge(S["q_lo"], 4 * g + h + 1)
                for t in range(TT):
                    last = pe.matmul(PG[:, t:t + 1], sqq[:, t * P:(t + 1) * P], ones[:, :], start=True, stop=True)
                last.then_inc(S["ss_mm"], 1)

            def wo_job(g, t):
                if t == 0:
                    pe.wait_ge(S["b_split"], g + 1)
                    pe.wait_ge(S["o_lo"], 4 * g + 4)
                m = 0
                for a, w in PASS:
                    for h in range(GRP):
                        last = pe.matmul(PG[:, :], oT[a][:, h, t * P:(t + 1) * P], wB[w][:, h, :],
                                         start=(m == 0), stop=(m == 11))
                        m += 1
                last.then_inc(S["wo_mm"], 1)

            def scores(g, s, n, first):
                h, t = s // 4, s % 4
                b = t // 2
                if not (first and s < 2):
                    pe.wait_ge(S["exp_done"], n - 1)
                if t == 0:
                    pe.wait_ge(S["q_lo"], 4 * g + h + 1)
                for m, (a, w) in enumerate(PASS):
                    pe.matmul(PS[s % 2][:, 0:SC], q[a][:, h, t * P:(t + 1) * P], kTc[w][:, g, b * SC:(b + 1) * SC],
                              start=(m == 0), stop=(m == 2))
                for m, (a, w) in enumerate(PASS):
                    last = pe.matmul(PS[s % 2][:, SC:KL], q[a][:, h, t * P:(t + 1) * P],
                                     kTx[w][:, g, b * KX:(b + 1) * KX], start=(m == 0), stop=(m == 2))
                last.then_inc(S["s_mm"], 1)

            def probs_T(s, n, first):
                pe.wait_ge(S["norm_done"], n - 1)
                if not (first and s < 3):
                    pe.wait_ge(S["pt_lo"], n - 2)
                for k in range(KT):
                    last = pe.transpose(PTT[:, k * P:(k + 1) * P], Pb[(s - 2) % 4][:, k * P:(k + 1) * P], ident[:, :])
                last.then_inc(S["t_done"], 1)

            def values(g, s, n, first):
                k4 = (s - 3) % SLOTS
                t = k4 % 4
                b = t // 2
                pe.wait_ge(S["pt_lo"], n - 2)
                if t == 0 and not (first and s == 3):
                    pe.wait_ge(S["o_lo"], 4 * g + k4 // 4)
                m = 0
                for w, a in PASS:
                    for k in range(KT):
                        v = Vc[w][:, b * 4 + k, bass.ts(g, HD)] if k < 4 else Vx[w][:, b * 2 + k - 4, bass.ts(g, HD)]
                        last = pe.matmul(PO[:, t * P:(t + 1) * P], v, pt[(s - 3) % 2][a][:, k, :],
                                         start=(m == 0), stop=(m == 3 * KT - 1))
                        m += 1
                last.then_inc(S["pv_done"], 1)

            def slot(g, s, first=False, final=False):
                n = SLOTS * g + s
                scores(g, s, n, first)
                if not (first and s < 2):
                    probs_T(s, n, first)
                if not (first and s < 3):
                    values(g if s >= 3 else g - 1, s, n, first)
                if s == 0:
                    ss_job(g, 3)
                if s in (3, 4, 5, 6) and not first:
                    if s == 3:
                        pe.wait_ge(S["ss_read"], 4 * g + 4)
                    else:
                        pe.wait_ge(S["wo_add"], 4 * g - 4 + s - 3)
                    wo_job(g - 1, s - 3)
                if not final:
                    if s in (9, 11, 13, 15):
                        h = (s - 9) // 2
                        if h == 0:
                            if first:
                                pe.wait_ge(S["ss_read"], 4)
                            else:
                                pe.wait_ge(S["wo_add"], 4 * g)
                        else:
                            pe.wait_ge(S["ss_read"], 4 * g + 4 + h)
                        q_job(g + 1, h)
                    if s in (10, 12, 14):
                        ss_job(g + 1, (s - 10) // 2)

            pe.wait_ge(S["k_lo"], 2 * (CT + TT) + 1)
            pe.wait_ge(S["v_lo"], 2 * (CT + TT) + 2)
            for h in range(GRP):
                if h:
                    pe.wait_ge(S["ss_read"], h)
                q_job(0, h)
                if h < GRP - 1:
                    ss_job(0, h)
            for s in range(SLOTS):
                slot(0, s, first=True)
            with pe.Fori(1, KVH - 1) as g:
                for s in range(SLOTS):
                    slot(g, s)
            for s in range(SLOTS):
                slot(KVH - 1, s, final=True)
            for s in range(3):
                n = SLOTS * KVH + s
                if s < 2:
                    probs_T(s, n, False)
                values(KVH - 1, s, n, False)
            for t in range(TT):
                pe.wait_ge(S["wo_add"], 4 * (KVH - 1) + t)
                wo_job(KVH - 1, t)
            xT_transpose(1)
            pe.wait_ge(S["xT_f"], HC)
            pe.wait_ge(S["ld_small"], 16 * 9)
            for t in range(TT):
                for c in range(HC):
                    last = pe.matmul(fbank[0][:, t * NE:(t + 1) * NE], x2T[:, c, t * P:(t + 1) * P], wg_s[:, c, :],
                                     start=(c == 0), stop=(c == HC - 1))
                last.then_inc(S["lg_mm"], 1)
            pe.wait_ge(S["lg_b"], TT)
            pe.wait_ge(S["xT_lo"], 2 * HC)

            def expert(ep, u, first=False):
                pe.wait_ge(S[("a_split", "b_split")[u]], KVH + 1 + ep)
                w = (wA, wB)[u]
                for t in range(TT):
                    if not (first and u == 0):
                        pe.wait_ge(S["z_done"], 8 * ep + 4 * u + t - 3)
                    m = 0
                    for a, l in PASS:
                        for c in range(HC):
                            last = pe.matmul(fbank[t], xh[a][:, c, t * P:(t + 1) * P], w[l][:, c, :],
                                             start=(m == 0), stop=(m == 11))
                            m += 1
                    last.then_inc(S["f_mm"], 1)
            expert(0, 0, first=True)
            expert(0, 1)
            with pe.Fori(1, NE // 2) as ep:
                expert(ep, 0)
                expert(ep, 1)


def flat(a):
    return a.rearrange("p c t -> p (c t)")


def kernel(x, ctx_4096, L0_attn_A_log, L0_attn_D, L0_attn_x_proj_w, L0_attn_dt_proj_w, L0_attn_dt_proj_b,
           L0_xattn_Wq, L0_xattn_Wk, L0_xattn_Wv, L0_xattn_Wo, L0_xattn_q_norm_w, L0_xattn_k_norm_w,
           L0_ffn_W_gate, L0_ffn_b_gate, L0_ffn_W_e, L0_ffn_b_e):
    import numpy as np
    import concourse.bacc as bacc
    from concourse.bass_utils import run_bass_kernel_spmd

    def a(v):
        return np.asarray(v)

    def chunked(w, cols):
        w = a(w)
        return w.reshape(HC, P, -1, cols).transpose(2, 1, 0, 3)

    wk, wv = chunked(L0_xattn_Wk, DM), chunked(L0_xattn_Wv, DM)
    ctx_t = a(ctx_4096).reshape(CT, P, HC, P).transpose(0, 3, 2, 1)
    pieces = np.concatenate([wk.transpose(0, 2, 1, 3).reshape(8, P, DM), ctx_t.reshape(CT, P, DM),
                             wv.transpose(0, 2, 1, 3).reshape(8, P, DM)])
    wq = chunked(L0_xattn_Wq, GRP * HD)
    wo = a(L0_xattn_Wo).reshape(KVH, GRP, HD, DM).transpose(0, 2, 1, 3)
    we = a(L0_ffn_W_e).reshape(NE, HC, P, DM).transpose(0, 2, 1, 3)
    arrays = {
        "xT": a(x).reshape(NT, DM).T,
        "pieces": pieces,
        "wx": a(L0_attn_x_proj_w).T,
        "wdt": a(L0_attn_dt_proj_w).T,
        "dtb": a(L0_attn_dt_proj_b).reshape(HC, P).T,
        "alog": a(L0_attn_A_log).reshape(HC, P, NS).transpose(1, 0, 2).reshape(P, HC * NS),
        "dskip": a(L0_attn_D).reshape(HC, P).T,
        "qnw": a(L0_xattn_q_norm_w).reshape(HD, 1),
        "knw": a(L0_xattn_k_norm_w).reshape(HD, 1),
        "wa": np.concatenate([wq, we[0::2]]),
        "wb": np.concatenate([wo, we[1::2]]),
        "wg": a(L0_ffn_W_gate),
        "bg": a(L0_ffn_b_gate),
        "be": a(L0_ffn_b_e),
    }
    nc = bacc.Bacc("TRN2", target_bir_lowering=False, num_devices=1)
    arrays = {k: np.ascontiguousarray(v) for k, v in arrays.items()}
    args = {k: nc.dram_tensor(k, v.shape, mybir.dt.from_np(v.dtype), kind="ExternalInput").ap() for k, v in arrays.items()}
    args["scratch"] = nc.dram_tensor("scratch", (2 * NS, NT), fp32).ap()
    args["out"] = nc.dram_tensor("out", (TT, P, DM), fp32, kind="ExternalOutput").ap()
    decoder_layer(nc, **args)
    r = run_bass_kernel_spmd(nc, [arrays], core_ids=[0])
    return np.asarray(r.results[0]["out"]).reshape(NB, SX, DM)
```

```python
import concourse.bass as bass
from concourse import mybir
from contextlib import ExitStack

fp32 = mybir.dt.float32
fp16 = mybir.dt.float16
u32 = mybir.dt.uint32
ALU = mybir.AluOpType
ACT = mybir.ActivationFunctionType
AX = mybir.AxisListType

P = 128
NB, SX, SC, DM = 2, 256, 512, 512
NT = NB * SX
TT = NT // P
CT = NB * SC // P
HC = DM // P
NS, DTR = 16, 16
NCH = 4
NPC = NS // NCH
KVH, HD, GRP = 8, 128, 4
KX = SX
KL = SC + SX
KT = KL // P
SLOTS = GRP * TT
NE = 8
RMS_EPS, LN_EPS = 1e-6, 1e-5
PIECES = 8 + CT + 8
PC_K, PC_V = 0, 12
PC_C = (8, 16)
SLOT_LD = 4


def decoder_layer(nc, xT, pieces, wx, wdt, dtb, alog, dskip, qnw, knw, wa, wb,
                  wg, bg, be, scratch, out):
    ctx = ExitStack()
    with ctx:
        def sb(name, shape, dt=fp32):
            return ctx.enter_context(nc.sbuf_tensor(name, shape, dt))

        def sem(name):
            return ctx.enter_context(nc.semaphore(name))

        class Arena:
            def __init__(self, name, kbytes):
                self.t, self.at, self.size = sb(name, [P, kbytes * 256]), 0, kbytes * 256

            def view(self, words, dt=fp32):
                v = self.t[:, self.at:self.at + words]
                self.at += words
                assert self.at <= self.size, (self.at, self.size)
                return v if dt == fp32 else v.bitcast(dt)

            def again(self):
                self.at = 0

        kTc = [sb(f"kTc_{s}", [P, KVH, NB * SC], fp16) for s in ("hi", "lo")]
        Vc = [sb(f"Vc_{s}", [P, CT, KVH * HD], fp16) for s in ("hi", "lo")]
        x1 = sb("x1", [P, TT, DM])
        ident = sb("ident", [P, P])
        ones = sb("ones", [P, 1])
        half = sb("half", [P, 8])
        dtb_s = sb("dtb_s", [P, HC])
        dsk_s = sb("dsk_s", [P, HC])
        A_s = sb("A_s", [P, HC * NS])
        qkw = sb("qkw", [P, 1])
        knw_s = sb("knw_s", [P, 1])
        xd = sb("xd", [P, SX])
        ssk = sb("ssk", [P, KVH])
        rk = sb("rk", [P, KVH])
        lnst = sb("lnst", [P, TT, 6])
        mv = sb("mv", [P, TT, 2])
        rstd = sb("rstd", [P, TT])
        mx = sb("mx", [P, SLOTS])
        negb = sb("negb", [P, SLOTS])
        lsum = sb("lsum", [P, SLOTS])
        rl = sb("rl", [P, SLOTS])
        ssq = sb("ssq", [P, GRP, TT])
        cq = sb("cq", [P, GRP, TT])
        wg_s = sb("wg_s", [P, HC, NE])
        bg_s = sb("bg_s", [P, NE])
        iot = sb("iot", [P, NE])
        RA = Arena("RA", 48)
        pc = [RA.view(PIECES * 256, fp16).rearrange("p (k n) -> p k n", k=PIECES) for _ in range(2)]
        RA.again()
        q = [RA.view(GRP * NT // 2, fp16).rearrange("p (h n) -> p h n", h=GRP) for _ in range(2)]
        sqq = RA.view(NT)
        pt = [[RA.view(KL // 2, fp16).rearrange("p (k n) -> p k n", k=KT) for _ in range(2)] for _ in range(2)]
        oT = [RA.view(GRP * NT // 2, fp16).rearrange("p (h n) -> p h n", h=GRP) for _ in range(2)]
        be_s = RA.view(NE * DM).rearrange("p (e n) -> p e n", e=NE)
        zb = [RA.view(DM) for _ in range(2)]
        rb = [RA.view(DM) for _ in range(2)]
        RB = Arena("RB", 84)
        Bb = RB.view(NS * SX).rearrange("p (n t) -> p n t", n=NS)
        Cb = RB.view(NS * SX).rearrange("p (n t) -> p n t", n=NS)
        xT_s = RB.view(HC * NT).rearrange("p (c t) -> p c t", c=HC)
        dA = [RB.view(NPC * SX) for _ in range(2)]
        W = [RB.view(NPC * SX) for _ in range(NCH)]
        stg = [RB.view(DM) for _ in range(SLOT_LD)]
        dt_s = RB.view(NB * HC * SX).rearrange("p (j t) -> p j t", j=NB * HC)
        kn = [RB.view(DM) for _ in range(2)]
        u_s = Vc[1][:, CT - 1, 0:512].bitcast(fp32)
        wdt_s, xp_s, wx_s = kn[0], kn[1], u_s[:, 0:HC * 48].rearrange("p (c r) -> p c r", c=HC)
        dA_all = RB.t[:, 2 * NS * SX + HC * NT:2 * NS * SX + HC * NT + 2 * NPC * SX]
        x1_all = x1[:, :, :].rearrange("p t n -> p (t n)")
        HW = HC * SX
        sp_e = [dA_all[:, 0:HW], x1_all[:, 0:HW]]
        sp_l = [dA_all[:, HW:2 * HW], x1_all[:, HW:2 * HW]]
        sp_u = [Vc[0][:, 4 + 2 * b:6 + 2 * b, :].rearrange("p k n -> p (k n)").bitcast(fp32) for b in range(NB)]
        RB.again()
        kTx = [RB.view(KVH * NT // 2, fp16).rearrange("p (h n) -> p h n", h=KVH) for _ in range(2)]
        Vx = [RB.view(TT * 512, fp16).rearrange("p (k n) -> p k n", k=TT) for _ in range(2)]
        xh = [RB.view(HC * NT // 2, fp16).rearrange("p (c t) -> p c t", c=HC) for _ in range(2)]
        wA = [RB.view(HC * DM // 2, fp16).rearrange("p (c n) -> p c n", c=HC) for _ in range(2)]
        wA_f = RB.view(HC * DM).rearrange("p (c n) -> p c n", c=HC)
        wB = [RB.view(HC * DM // 2, fp16).rearrange("p (c n) -> p c n", c=HC) for _ in range(2)]
        wB_f = RB.view(HC * DM).rearrange("p (c n) -> p c n", c=HC)
        Pb_at = RB.at
        Pb = [RB.view(KL) for _ in range(4)]
        RB.at = Pb_at
        x2T = RB.view(HC * NT).rearrange("p (c t) -> p c t", c=HC)
        lgt, top, wsel, wtmp = (RB.view(TT * NE).rearrange("p (t e) -> p t e", t=TT) for _ in range(4))
        tix = RB.view(TT * NE, u32).rearrange("p (t e) -> p t e", t=TT)
        tixf = RB.view(TT * 2).rearrange("p (t e) -> p t e", t=TT)

        def pb(name, banks):
            return ctx.enter_context(nc.psum_tensor(name, [P, banks * 512], fp32))
        PS = [pb("PS0", 2), pb("PS1", 2)]
        PTT, PO, PG = pb("PTT", 2), pb("PO", 1), pb("PG", 1)
        kvp = [PS[0][:, 0:512], PS[0][:, 512:1024], PO[:, :], PG[:, :]]
        ktp = [PS[1][:, 0:512], PS[1][:, 512:1024]]
        yp = PTT[:, :].rearrange("p (t n) -> p t n", t=2)[:, :, 0:P]
        dtp = [[PTT[:, c * SX:(c + 1) * SX] for c in range(HC)],
               [PS[1][:, 512:768], PS[1][:, 768:1024], PG[:, 0:SX], PG[:, SX:2 * SX]]]
        four = [PO[:, :], PG[:, :], PTT[:, 0:512], PTT[:, 512:1024]]
        q0b = [PO[:, :], PTT[:, 0:512], PTT[:, 512:1024], PG[:, :]]
        fbank = [PS[0][:, 0:512], PS[0][:, 512:1024], PS[1][:, 0:512], PS[1][:, 512:1024]]

        S = {n: sem(n) for n in (
            "ld_wx", "ld_small", "ld_be", "const_ready", "xp_mm", "xp_sb", "bc_out", "dtl_mm", "sp_abs",
            "sp_exp", "sp_ln", "sp_diff", "sp_max", "sp_inv", "sp_v", "A_exp", "A_ready", "qkw_ready", "split_v", "split_p", "dt_ready",
            "split_hi_v", "split_hi_p",
            "zero_ready", "xd_ready", "u_ready", "dA_ready", "dBx_ready", "h_ready", "g_ready", "pair_added_v", "pair_added_p", "y_mm",
            "r_ev", "kv_mm", "k_sq", "rk_tmp", "k_r", "k_n", "k_tr", "k_hi", "k_lo", "v_hi", "v_lo",
            "ln_st", "ln_mv", "ln_eps", "ln_rstd", "ln_x", "xT_tr", "xT_hi", "xT_lo", "xT_f",
            "a_ld", "a_hi", "a_split", "b_ld", "b_hi", "b_split",
            "s_mm", "mx_done", "negb_done", "exp_done", "rl_done", "norm_done", "t_done", "pt_hi", "pt_lo", "pv_done",
            "o_hi", "o_lo", "wo_mm", "wo_add", "q_mm", "q_hi", "q_sq", "q_lo", "ss_mm", "ss_read", "cq_done",
            "lg_mm", "lg_b", "lg_top", "lg_ix", "lg_f", "lg_eq", "lg_w", "f_mm", "z_done", "relu_done", "acc_done",
            "o_dma", "pool_waited")}
        x_ld = [sem(f"x_ld{c}") for c in range(HC)]
        pc_ld = [sem(f"pc_ld{k}") for k in range(SLOT_LD)]
        bc_ld = [sem(f"bc_ld{c}") for c in range(NCH)]
        N_SMALL = 8
        block = ctx.enter_context(nc.Block())

        def bc_chunk(b, c):
            for dst, row in ((Bb, 0), (Cb, NS)):
                src = scratch[row + c * NPC:row + (c + 1) * NPC, b * SX:(b + 1) * SX]
                nc.sync.dma_start(dst[:, c * NPC:(c + 1) * NPC, :], src.partition_broadcast(P)).then_inc(bc_ld[c], 16)

        @block.sync
        def _(sp):
            for c in range(HC):
                sp.dma_start(xT_s[:, c, :], xT[c * P:(c + 1) * P, :]).then_inc(x_ld[c], 16)

            def piece(i, k):
                sp.dma_start(stg[k], pieces[i * SLOT_LD + k, :, :]).then_inc(pc_ld[k], 16)

            for k in range(SLOT_LD):
                piece(0, k)

            def refill(i):
                for k in range(SLOT_LD):
                    sp.wait_ge(S["split_v"] if k < 2 else S["split_p"], 2 * i - 1 + k % 2)
                    piece(i, k)
            refill(1)
            sp.wait_ge(S["xp_sb"], 1)
            sp.dma_start(scratch, xp_s[DTR:DTR + 2 * NS, :]).then_inc(S["bc_out"], 16)
            refill(2)
            sp.wait_ge(S["bc_out"], 16)
            for c in range(NCH):
                bc_chunk(0, c)
            with sp.Fori(3, PIECES // SLOT_LD) as i:
                refill(i)
            for c in range(NCH):
                sp.wait_ge(S["g_ready"], HC * NCH - NCH + c + 1)
                bc_chunk(1, c)
            sp.wait_ge(S["r_ev"], NB * HC + 1)
            sp.dma_start(wA_f, wa[0]).then_inc(S["a_ld"], 16)
            sp.dma_start(wB_f, wb[0]).then_inc(S["b_ld"], 16)
            sp.wait_ge(S["kv_mm"], 4 * (CT + TT))
            sp.dma_start(be_s, be.partition_broadcast(P)).then_inc(S["ld_be"], 16)
            with sp.Fori(1, KVH + NE // 2) as i:
                sp.wait_ge(S["a_split"], i)
                sp.dma_start(wA_f, wa[i]).then_inc(S["a_ld"], 16)
                sp.wait_ge(S["b_split"], i)
                sp.dma_start(wB_f, wb[i]).then_inc(S["b_ld"], 16)
            for t in range(TT):
                sp.wait_ge(S["ln_x"], 2 * TT + t + 1)
                sp.dma_start(out[t], x1[:, t, :]).then_inc(S["o_dma"], 16)
            sp.wait_ge(S["o_dma"], 16 * TT)

        @block.gpsimd
        def _(pool):
            pool.memset(ident[:, :], 0.0).then_inc(S["const_ready"], 1)
            pool.wait_ge(S["const_ready"], 1)
            pool.affine_select(out=ident[:, :], in_=ident[:, :], compare_op=ALU.not_equal, fill=1.0, base=0,
                               pattern=[[-1, P]], channel_multiplier=1).then_inc(S["const_ready"], 1)
            pool.memset(ones[:, :], 1.0).then_inc(S["const_ready"], 1)
            pool.memset(half[:, :], -0.5).then_inc(S["const_ready"], 1)
            for e in range(NE):
                pool.memset(iot[:, e:e + 1], float(e)).then_inc(S["const_ready"], 1)

            def waited():
                pool.sem_inc(S["pool_waited"], 1)

            def hi_lo(src, hi, lo, s_hi, n, s_lo):
                pool.tensor_scalar(hi, src, 1.0, 1.0, ALU.mult, ALU.mult).then_inc(s_hi, 1)
                pool.wait_ge(s_hi, n + 1)
                pool.tensor_tensor(lo, src, hi, ALU.subtract).then_inc(s_lo, 1)

            def split(i):
                for k in (2, 3):
                    pool.wait_ge(pc_ld[k], 16 * i + 16)
                    hi_lo(stg[k], pc[0][:, i * SLOT_LD + k, :], pc[1][:, i * SLOT_LD + k, :],
                          S["split_hi_p"], 2 * i + k - 2, S["split_p"])

            def rk_of(j):
                pool.wait_ge(S["k_sq"], 2 * j + 2)
                waited()
                pool.tensor_scalar(rk[:, :], ssk[:, :], 1.0 / HD, RMS_EPS, ALU.mult, ALU.add).then_inc(S["rk_tmp"], 1)
                pool.wait_ge(S["rk_tmp"], j + 1)
                pool.tensor_tensor(rk[:, :], rk[:, :], half[:, :], ALU.pow).then_inc(S["k_r"], 1)

            def scan_step(b, i, first=False):
                j = i + HC * b
                pool.tensor_tensor(u_s, dt_s[:, j, :], xT_s[:, i, b * SX:(b + 1) * SX], ALU.mult)\
                    .then_inc(S["u_ready"], 1)
                for c in range(NCH):
                    pool.wait_ge(bc_ld[c], 32 * (b + 1))
                    if c == 0:
                        pool.wait_ge(S["u_ready"], j + 1)
                    if c % 2:
                        pool.wait_ge(S["y_mm"], 2 * j + c // 2 + 1)
                    elif not first:
                        pool.wait_ge(S["pair_added_p"] if c else S["pair_added_v"], j)
                    ub = u_s.unsqueeze(1).broadcast_to([P, NPC, SX])
                    pool.tensor_tensor(W[c].rearrange("p (n t) -> p n t", n=NPC), Bb[:, c * NPC:(c + 1) * NPC, :],
                                       ub, ALU.mult).then_inc(S["dBx_ready"], 1)
                    if c == 2:
                        rk_of(j)
                if first:
                    split(3)
                    split(4)
                    split(5)
                pool.wait_ge(S["g_ready"], NCH * j + NCH)
                pool.tensor_tensor(W[3], W[3], W[2], ALU.add).then_inc(S["pair_added_p"], 1)

            for i in range(3):
                split(i)
            pool.wait_ge(S["dt_ready"], 1)
            scan_step(0, 0, first=True)
            with pool.Fori(1, HC) as i:
                scan_step(0, i)
            pool.wait_ge(S["dt_ready"], 2)
            with pool.Fori(0, HC) as i:
                scan_step(1, i)

            def w_piece(s, i, c, free=None):
                if free:
                    pool.wait_ge(*free)
                f, w, ld, h, sp_ = ((wA_f, wA, "a_ld", "a_hi", "a_split"), (wB_f, wB, "b_ld", "b_hi", "b_split"))[s]
                if c == 0:
                    pool.wait_ge(S[ld], 16 * i + 16)
                    waited()
                pool.tensor_scalar(w[0][:, c, :], f[:, c, :], 1.0, 1.0, ALU.mult, ALU.mult).then_inc(S[h], 1)
                pool.wait_ge(S[h], 4 * i + c + 1)
                last = pool.tensor_tensor(w[1][:, c, :], f[:, c, :], w[0][:, c, :], ALU.subtract)
                if c == HC - 1:
                    last.then_inc(S[sp_], 1)

            def ln_rstd(k):
                pool.wait_ge(S["ln_mv"], TT * (k + 1))
                pool.tensor_scalar(rstd[:, :], mv[:, :, 1], LN_EPS, 1.0, ALU.add, ALU.mult).then_inc(S["ln_eps"], 1)
                pool.wait_ge(S["ln_eps"], k + 1)
                pool.tensor_tensor(rstd[:, :], rstd[:, :], half[:, 0:TT], ALU.pow).then_inc(S["ln_rstd"], 1)

            ln_rstd(0)
            pool.wait_ge(S["y_mm"], 2 * NB * HC + 2)
            for c in range(HC):
                w_piece(0, 0, c)
            with pool.Fori(CT, CT + TT) as j:
                rk_of(j)

            def cq_of(n):
                h = n[1]
                pool.wait_ge(S["ss_read"], 4 * n[0] + h + 1)
                pool.tensor_tensor(cq[:, h, :], ssq[:, h, :], half[:, 0:TT], ALU.pow).then_inc(S["cq_done"], 1)

            for h in range(GRP - 1):
                cq_of((0, h))

            def slot(g, s, first=False, last=False):
                n = SLOTS * g + s
                if not (first and s == 0):
                    pool.wait_ge(S["rl_done"], n)
                    k = (s - 1) % SLOTS
                    waited()
                    pool.tensor_scalar(Pb[(s - 1) % 4], Pb[(s - 1) % 4], rl[:, k:k + 1], 1.0, ALU.mult, ALU.mult)\
                        .then_inc(S["norm_done"], 1)
                if last:
                    return
                if s == 0:
                    if not first:
                        pool.wait_ge(S["exp_done"], n)
                    cq_of((g, 3))
                if s in (1, 3, 5, 7):
                    w_piece(0, g + 1, s // 2, (S["q_mm"], 4 * g + 4) if s == 1 else None)
                if s in (8, 10, 12, 14):
                    w_piece(1, g, s // 2 - 4, (S["wo_mm"], 4 * g) if s == 8 and not first else None)

            def body(g, first=False, final=False):
                for s in range(SLOTS):
                    slot(g, s, first)
                    if not final and s in (10, 12, 14):
                        cq_of((g + 1, s // 2 - 5))

            body(0, first=True)
            with pool.Fori(1, KVH - 1) as g:
                body(g)
            body(KVH - 1, final=True)
            slot(KVH, 0, last=True)
            ln_rstd(1)
            pool.wait_ge(S["wo_mm"], 4 * KVH)
            for c in range(HC):
                w_piece(1, KVH, c)
            with pool.Fori(1, NE // 2) as k:
                for c in range(HC):
                    w_piece(0, KVH + k, c, (S["f_mm"], 8 * k - 4) if c == 0 else None)
                for c in range(HC):
                    w_piece(1, KVH + k, c, (S["f_mm"], 8 * k) if c == 0 else None)
            ln_rstd(2)

        @block.scalar
        def _(act):
            act.dma_start(wx_s, wx.rearrange("(c p) r -> p c r", p=P)).then_inc(S["ld_wx"], 16)
            small = [(wdt_s[0:DTR, :], wdt), (dtb_s[:, :], dtb),
                     (A_s[:, :], alog), (dsk_s[:, :], dskip), (qkw[:, :], qnw), (knw_s[:, :], knw),
                     (wg_s[:, :, :], wg.rearrange("(c p) e -> p c e", p=P)), (bg_s[:, :], bg.partition_broadcast(P))]
            assert len(small) == N_SMALL
            for dst, src in small:
                act.dma_start(dst, src).then_inc(S["ld_small"], 16)
            act.wait_ge(S["xp_mm"], 1)
            act.activation(xp_s[0:48, :], PS[1][0:48, 512:1024], ACT.Copy).then_inc(S["xp_sb"], 1)
            act.wait_ge(S["ld_small"], 16 * N_SMALL)
            act.activation(A_s[:, :], A_s[:, :], ACT.Exp).then_inc(S["A_exp"], 1)
            for b in range(NB):
                act.wait_ge(S["dtl_mm"], HC * (b + 1))
                for c in range(HC):
                    act.activation(dt_s[:, HC * b + c, :], dtp[b][c], ACT.Abs, bias=dtb_s[:, c:c + 1])\
                        .then_inc(S["sp_abs"], 1)
            for b in range(NB):
                act.wait_ge(S["sp_abs"], HC * (b + 1))
                act.activation(sp_e[b], flat(dt_s[:, HC * b:HC * b + HC, :]), ACT.Exp, scale=-1.0)\
                    .then_inc(S["sp_exp"], 1)
            for b in range(NB):
                act.wait_ge(S["sp_exp"], b + 1)
                act.activation(sp_l[b], sp_e[b], ACT.Ln, bias=1.0).then_inc(S["sp_ln"], 1)
            for b in range(NB):
                act.wait_ge(S["sp_ln"], b + 1)
                act.wait_ge(S["sp_diff"], b + 1)
                act.activation(sp_e[b], sp_l[b], ACT.Exp, scale=-1.0).then_inc(S["sp_inv"], 1)
            act.wait_ge(S["A_ready"], 1)
            act.wait_ge(S["zero_ready"], 2)

            def exps(j, c):
                i = j[1]
                j = j[0]
                act.wait_ge(S["h_ready"], NCH * j + c + 1)
                for n in range(NPC):
                    last = act.activation(dA[c % 2][:, n * SX + 1:(n + 1) * SX], dt_s[:, j, 1:SX],
                                          ACT.Exp, scale=A_s[:, bass.ds(i * NS + c * NPC + n, 1)])
                last.then_inc(S["dA_ready"], 1)

            def k_square(j, blk):
                act.wait_ge(S["kv_mm"], 4 * j + blk + 1)
                act.wait_ge(S["k_tr"], 2 * j + blk + 1)
                for h in range(4):
                    last = act.activation(kn[blk][:, h * HD:(h + 1) * HD], kvp[blk][:, h * HD:(h + 1) * HD], ACT.Square,
                                          accum_out=ssk[:, 4 * blk + h:4 * blk + h + 1])
                last.then_inc(S["k_sq"], 1)

            def k_high(j, blk, dst):
                act.wait_ge(S["k_tr"], 2 * j + blk + 3)
                act.activation(dst, ktp[blk].rearrange("p (h t) -> p h t", h=4), ACT.Copy, scale=qkw[:, 0:1])\
                    .then_inc(S["k_hi"], 1)

            def v_high(j, blk, dst):
                act.wait_ge(S["kv_mm"], 4 * j + 2 + blk + 1)
                act.activation(dst, kvp[2 + blk], ACT.Copy).then_inc(S["v_hi"], 1)

            act.wait_ge(S["qkw_ready"], 2)
            act.wait_ge(S["dt_ready"], 1)

            def y_evac(b, i):
                act.wait_ge(S["y_mm"], 2 * (i + HC * b) + 4)
                act.activation(x1[:, 2 * b:2 * b + 2, bass.ts(i, P)], yp, ACT.Copy).then_inc(S["r_ev"], 1)

            def scan_step(b, i, former):
                j = i + HC * b
                kd = [kTc[0][:, 4 * k:4 * k + 4, bass.ts(j, P)] for k in range(2)]
                vd = [Vc[0][:, j, 512 * k:512 * k + 512] for k in range(2)]
                exps((j, i), 0)
                exps((j, i), 1)
                if former:
                    y_evac(*former)
                act.activation(xd[:, :], xT_s[:, i, b * SX:(b + 1) * SX], ACT.Copy, scale=dsk_s[:, bass.ds(i, 1)])\
                    .then_inc(S["xd_ready"], 1)
                k_square(j, 0)
                exps((j, i), 2)
                k_square(j, 1)
                exps((j, i), 3)
                v_high(j, 0, vd[0])
                v_high(j, 1, vd[1])
                k_high(j, 0, kd[0])
                k_high(j, 1, kd[1])

            scan_step(0, 0, None)
            with act.Fori(1, HC) as i:
                scan_step(0, i, (0, i - 1))
            act.wait_ge(S["dt_ready"], 2)
            scan_step(1, 0, (0, HC - 1))
            with act.Fori(1, HC) as i:
                scan_step(1, i, (1, i - 1))
            y_evac(1, HC - 1)

            def xT_high(k, wide):
                for c in range(HC):
                    act.wait_ge(S["xT_tr"], HC * k + c + 1)
                    if wide:
                        act.activation(x2T[:, c, :], four[c], ACT.Copy).then_inc(S["xT_f"], 1)
                    act.activation(xh[0][:, c, :], four[c], ACT.Copy).then_inc(S["xT_hi"], 1)

            xT_high(0, False)
            with act.Fori(0, TT) as t:
                j = t + CT
                for blk in range(2):
                    k_square(j, blk)
                for blk in range(2):
                    v_high(j, blk, Vx[0][:, t, 512 * blk:512 * blk + 512])
                    k_high(j, blk, kTx[0][:, 4 * blk:4 * blk + 4, bass.ts(t, P)])

            def q_evac(g, h, bank=PG, first=False):
                n = 4 * g + h
                act.wait_ge(S["q_mm"], n + 1)
                act.activation(q[0][:, h, :], bank[:, :], ACT.Copy).then_inc(S["q_hi"], 1)
                if not (first and h == 0):
                    act.wait_ge(S["ss_mm"], n)
                act.activation(sqq, bank[:, :], ACT.Square).then_inc(S["q_sq"], 1)

            def slot(g, s, first=False, final=False):
                n = SLOTS * g + s
                if not (first and s < 2):
                    act.wait_ge(S["t_done"], n - 1)
                    if not (first and s < 4):
                        act.wait_ge(S["pv_done"], n - 3)
                    act.activation(pt[s % 2][0], PTT[:, 0:KL].rearrange("p (k n) -> p k n", k=KT), ACT.Copy)\
                        .then_inc(S["pt_hi"], 1)
                act.wait_ge(S["negb_done"], n + 1)
                if not (first and s < 4):
                    act.wait_ge(S["t_done"], n - 3)
                h, t = s // 4, s % 4
                act.activation(Pb[s % 4], PS[s % 2][:, 0:KL], ACT.Exp, scale=cq[:, h, t:t + 1],
                               bias=negb[:, s:s + 1], accum_out=lsum[:, s:s + 1]).then_inc(S["exp_done"], 1)
                if s % 4 == 2 and not (first and s == 2):
                    h = (s // 4 - 1) % 4
                    act.wait_ge(S["pv_done"], n - 2)
                    if s > 2 and not first:
                        act.wait_ge(S["wo_mm"], 4 * g)
                    act.activation(oT[0][:, h, :], PO[:, :], ACT.Copy).then_inc(S["o_hi"], 1)
                if not final and s in (9, 11, 13, 15):
                    q_evac(g + 1, (s - 9) // 2)

            act.wait_ge(S["kv_mm"], 4 * (CT + TT))
            for h in range(GRP):
                q_evac(0, h, q0b[h], first=True)
            for s in range(SLOTS):
                slot(0, s, first=True)
            with act.Fori(1, KVH - 1) as g:
                for s in range(SLOTS):
                    slot(g, s)
            for s in range(SLOTS):
                slot(KVH - 1, s, final=True)
            for s in range(3):
                n = SLOTS * KVH + s
                if s < 2:
                    act.wait_ge(S["t_done"], n - 1)
                    act.wait_ge(S["pv_done"], n - 3)
                    act.activation(pt[s % 2][0], PTT[:, 0:KL].rearrange("p (k n) -> p k n", k=KT), ACT.Copy)\
                        .then_inc(S["pt_hi"], 1)
                else:
                    act.wait_ge(S["pv_done"], n - 2)
                    act.activation(oT[0][:, 3, :], PO[:, :], ACT.Copy).then_inc(S["o_hi"], 1)
            xT_high(1, True)

            def relu(ep, u, t, first=False):
                J = 8 * ep + 4 * u + t
                act.wait_ge(S["z_done"], J + 1)
                if not (first and u == 0 and t < 2):
                    act.wait_ge(S["acc_done"], J - 1)
                act.activation(rb[t % 2], zb[t % 2], ACT.Relu, scale=wsel[:, t, bass.ds(2 * ep + u, 1)])\
                    .then_inc(S["relu_done"], 1)

            act.wait_ge(S["lg_w"], 1)
            for u in range(2):
                for t in range(TT):
                    relu(0, u, t, first=True)
            with act.Fori(1, NE // 2) as ep:
                for u in range(2):
                    for t in range(TT):
                        relu(ep, u, t)

        @block.vector
        def _(dve):
            def split(i, k):
                dve.wait_ge(pc_ld[k], 16 * i + 16)
                dve.tensor_copy(pc[0][:, i * SLOT_LD + k, :], stg[k]).then_inc(S["split_hi_v"], 1)
                dve.wait_ge(S["split_hi_v"], 2 * i + k + 1)
                dve.tensor_tensor(pc[1][:, i * SLOT_LD + k, :], stg[k], pc[0][:, i * SLOT_LD + k, :], ALU.subtract)\
                    .then_inc(S["split_v"], 1)

            dve.wait_ge(S["ld_small"], 16 * N_SMALL)
            dve.tensor_tensor(qkw[:, :], qkw[:, :], knw_s[:, :], ALU.mult).then_inc(S["qkw_ready"], 1)
            dve.tensor_scalar(dsk_s[:, :], dsk_s[:, :], 1.0, None, ALU.add).then_inc(S["qkw_ready"], 1)
            for i in range(3):
                split(i, 0)
                split(i, 1)
            dve.wait_ge(S["A_exp"], 1)
            dve.tensor_scalar(A_s[:, :], A_s[:, :], -1.0, None, ALU.mult).then_inc(S["A_ready"], 1)
            v = [0]

            def step(ins):
                v[0] += 1
                ins.then_inc(S["sp_v"], 1)
                dve.wait_ge(S["sp_v"], v[0])

            for b in range(NB):
                dve.wait_ge(S["sp_exp"], b + 1)
                dve.tensor_scalar(sp_u[b], sp_e[b], 1.0, None, ALU.add).then_inc(S["sp_v"], 1)
                dve.wait_ge(S["sp_v"], b + 1)
                dve.scalar_tensor_tensor(sp_u[b], sp_u[b], -1.0, sp_e[b], ALU.add, ALU.subtract).then_inc(S["sp_diff"], 1)
            for b in range(NB):
                for c in range(HC):
                    dve.tensor_scalar(dt_s[:, HC * b + c, :], dtp[b][c], dtb_s[:, c:c + 1], 0.0, ALU.add, ALU.max)\
                        .then_inc(S["sp_max"], 1)
            for b in range(NB):
                e, l, u = sp_e[b], sp_l[b], sp_u[b]
                d = flat(dt_s[:, HC * b:HC * b + HC, :])
                dve.wait_ge(S["sp_inv"], b + 1)
                dve.tensor_tensor(u, u, e, ALU.mult).then_inc(S["sp_v"], 1)
                dve.wait_ge(S["sp_v"], NB + 2 * b + 1)
                dve.tensor_tensor(l, l, u, ALU.subtract).then_inc(S["sp_v"], 1)
                dve.wait_ge(S["sp_v"], NB + 2 * b + 2)
                dve.wait_ge(S["sp_max"], HC * (b + 1))
                dve.tensor_tensor(d, d, l, ALU.add).then_inc(S["dt_ready"], 1)
                if b == 0:
                    dve.wait_ge(S["dt_ready"], 1)
                    for k in range(2):
                        z = dA[k].rearrange("p (n t) -> p n t", n=NPC)[:, :, 0:1]
                        dve.memset(z, 0.0).then_inc(S["zero_ready"], 1)
                    dve.sem_inc(S["h_ready"], 2)

            def k_norm(j, blk):
                dve.wait_ge(S["k_r"], j + 1)
                dve.tensor_tensor(kn[blk].rearrange("p (h d) -> p h d", h=4), kvp[blk].rearrange("p (h d) -> p h d", h=4),
                                  rk[:, 4 * blk:4 * blk + 4].unsqueeze(2).broadcast_to([P, 4, HD]), ALU.mult).then_inc(S["k_n"], 1)

            def k_low(j, blk, hi, lo):
                dve.wait_ge(S["k_hi"], 2 * j + blk + 1)
                dve.scalar_tensor_tensor(lo, ktp[blk].rearrange("p (h t) -> p h t", h=4), qkw[:, 0:1], hi,
                                         ALU.mult, ALU.subtract).then_inc(S["k_lo"], 1)

            def v_low(j, blk, hi, lo):
                dve.wait_ge(S["v_hi"], 2 * j + blk + 1)
                dve.tensor_tensor(lo, kvp[2 + blk], hi, ALU.subtract).then_inc(S["v_lo"], 1)

            def scan_step(b, i, first=False):
                j = i + HC * b
                kd = [[kTc[w][:, 4 * k:4 * k + 4, bass.ts(j, P)] for w in range(2)] for k in range(2)]
                vd = [[Vc[w][:, j, 512 * k:512 * k + 512] for w in range(2)] for k in range(2)]

                def scan(c):
                    dve.wait_ge(S["dA_ready"], NCH * j + c + 1)
                    dve.wait_ge(S["dBx_ready"], NCH * j + c + 1)
                    dve.tensor_tensor_scan(W[c], dA[c % 2], W[c], 0.0, ALU.mult, ALU.add).then_inc(S["h_ready"], 1)
                    dve.wait_ge(S["h_ready"], NCH * j + c + 3)
                    dve.tensor_tensor(W[c], W[c], Cb[:, c * NPC:(c + 1) * NPC, :].rearrange("p n t -> p (n t)"),
                                      ALU.mult).then_inc(S["g_ready"], 1)

                def splits(g):
                    if first:
                        split(g, 0)
                        split(g, 1)
                scan(0)
                scan(1)
                dve.wait_ge(S["g_ready"], NCH * j + 2)
                dve.tensor_tensor(W[1], W[1], W[0], ALU.add).then_inc(S["pair_added_v"], 1)
                splits(3)
                scan(2)
                splits(4)
                k_norm(j, 0)
                k_norm(j, 1)
                scan(3)
                splits(5)
                v_low(j, 0, *vd[0])
                v_low(j, 1, *vd[1])
                k_low(j, 0, *kd[0])
                k_low(j, 1, *kd[1])

            scan_step(0, 0, first=True)
            with dve.Fori(1, HC) as i:
                scan_step(0, i)
            with dve.Fori(0, HC) as i:
                scan_step(1, i)

            def norm(k):
                for t in range(TT):
                    dve.bn_stats(lnst[:, t, :], x1[:, t, :]).then_inc(S["ln_st"], 1)
                for t in range(TT):
                    dve.wait_ge(S["ln_st"], TT * k + t + 1)
                    dve.bn_aggr(mv[:, t, :], lnst[:, t, :]).then_inc(S["ln_mv"], 1)
                dve.wait_ge(S["ln_rstd"], k + 1)
                dve.wait_ge(S["ln_mv"], TT * (k + 1))
                for t in range(TT):
                    dve.tensor_scalar(x1[:, t, :], x1[:, t, :], mv[:, t, 0:1], rstd[:, t:t + 1],
                                      ALU.subtract, ALU.mult).then_inc(S["ln_x"], 1)

            def xT_low(k):
                for c in range(HC):
                    dve.wait_ge(S["xT_hi"], HC * k + c + 1)
                    dve.tensor_tensor(xh[1][:, c, :], four[c], xh[0][:, c, :], ALU.subtract).then_inc(S["xT_lo"], 1)

            dve.wait_ge(S["r_ev"], NB * HC + 1)
            norm(0)
            xT_low(0)
            with dve.Fori(0, TT) as t:
                j = t + CT
                kd = [[kTx[w][:, 4 * k:4 * k + 4, bass.ts(t, P)] for w in range(2)] for k in range(2)]
                k_norm(j, 0)
                k_norm(j, 1)
                for blk in range(2):
                    v_low(j, blk, *[Vx[w][:, t, 512 * blk:512 * blk + 512] for w in range(2)])
                    k_low(j, blk, *kd[blk])

            def q_low(g, h, bank=PG):
                dve.wait_ge(S["q_hi"], 4 * g + h + 1)
                dve.wait_ge(S["q_sq"], 4 * g + h + 1)
                dve.tensor_tensor(q[1][:, h, :], bank[:, :], q[0][:, h, :], ALU.subtract).then_inc(S["q_lo"], 1)

            def ss_evac(g, h, bank=PG):
                dve.wait_ge(S["ss_mm"], 4 * g + h + 1)
                dve.tensor_scalar(ssq[:, h, :], bank[:, 0:TT], HD * RMS_EPS, None, ALU.add).then_inc(S["ss_read"], 1)

            def pt_low(n, s):
                dve.wait_ge(S["pt_hi"], n - 1)
                dve.tensor_tensor(pt[s % 2][1], PTT[:, 0:KL].rearrange("p (k n) -> p k n", k=KT), pt[s % 2][0],
                                  ALU.subtract).then_inc(S["pt_lo"], 1)

            def o_low(n, h):
                dve.wait_ge(S["o_hi"], n)
                dve.tensor_tensor(oT[1][:, h, :], PO[:, :], oT[0][:, h, :], ALU.subtract).then_inc(S["o_lo"], 1)

            def wo_add(g, t):
                dve.wait_ge(S["wo_mm"], 4 * g + t + 1)
                dve.tensor_tensor(x1[:, t, :], x1[:, t, :], PG[:, :], ALU.add).then_inc(S["wo_add"], 1)

            def recip(n, s):
                dve.wait_ge(S["exp_done"], n)
                k = (s - 1) % SLOTS
                dve.reciprocal(rl[:, k:k + 1], lsum[:, k:k + 1]).then_inc(S["rl_done"], 1)

            def slot(g, s, first=False, final=False):
                n = SLOTS * g + s
                if not (first and s == 0):
                    recip(n, s)
                dve.wait_ge(S["s_mm"], n + 1)
                dve.reduce_max(mx[:, s:s + 1], PS[s % 2][:, 0:KL], AX.X).then_inc(S["mx_done"], 1)
                if s % 4 == 0:
                    dve.wait_ge(S["cq_done"], 4 * g + s // 4 + 1)
                dve.wait_ge(S["mx_done"], n + 1)
                dve.scalar_tensor_tensor(negb[:, s:s + 1], mx[:, s:s + 1], -1.0, cq[:, s // 4, s % 4:s % 4 + 1],
                                         ALU.mult, ALU.mult).then_inc(S["negb_done"], 1)
                if not (first and s < 2):
                    pt_low(n, s)
                if s % 4 == 2 and not (first and s == 2):
                    o_low(4 * g + s // 4, (s // 4 - 1) % 4)
                if s == 0:
                    ss_evac(g, 3)
                if s in (3, 4, 5, 6) and not first:
                    wo_add(g - 1, s - 3)
                if not final:
                    if s in (9, 11, 13, 15):
                        q_low(g + 1, (s - 9) // 2)
                    if s in (10, 12, 14):
                        ss_evac(g + 1, (s - 10) // 2)

            dve.wait_ge(S["kv_mm"], 4 * (CT + TT))
            for h in range(GRP):
                q_low(0, h, q0b[h])
                if h:
                    ss_evac(0, h - 1, q0b[h - 1])
            for s in range(SLOTS):
                slot(0, s, first=True)
            with dve.Fori(1, KVH - 1) as g:
                for s in range(SLOTS):
                    slot(g, s)
            for s in range(SLOTS):
                slot(KVH - 1, s, final=True)
            recip(SLOTS * KVH, 0)
            for s in range(2):
                pt_low(SLOTS * KVH + s, s)
            o_low(4 * KVH, 3)
            for t in range(TT):
                wo_add(KVH - 1, t)
            dve.wait_ge(S["wo_add"], 4 * KVH)
            norm(1)
            xT_low(1)
            dve.wait_ge(S["const_ready"], 4 + NE)
            for t in range(TT):
                dve.wait_ge(S["lg_mm"], TT)
                dve.tensor_tensor(lgt[:, t, :], fbank[0][:, t * NE:(t + 1) * NE], bg_s[:, :], ALU.add)\
                    .then_inc(S["lg_b"], 1)
            for t in range(TT):
                dve.wait_ge(S["lg_b"], t + 1)
                dve.max(top[:, t, :], lgt[:, t, :]).then_inc(S["lg_top"], 1)
            for t in range(TT):
                dve.wait_ge(S["lg_top"], t + 1)
                dve.max_index(tix[:, t, :], top[:, t, :], lgt[:, t, :]).then_inc(S["lg_ix"], 1)
            dve.wait_ge(S["lg_ix"], TT)
            dve.tensor_copy(tixf[:, :, :], tix[:, :, 0:2]).then_inc(S["lg_f"], 1)
            dve.wait_ge(S["lg_f"], 1)
            for t in range(TT):
                dve.tensor_scalar(wsel[:, t, :], iot[:, :], tixf[:, t, 0:1], 0.5, ALU.is_equal, ALU.mult)\
                    .then_inc(S["lg_eq"], 1)
                dve.tensor_scalar(wtmp[:, t, :], iot[:, :], tixf[:, t, 1:2], 0.5, ALU.is_equal, ALU.mult)\
                    .then_inc(S["lg_eq"], 1)
            dve.wait_ge(S["lg_eq"], 2 * TT)
            dve.tensor_tensor(wsel[:, :, :], wsel[:, :, :], wtmp[:, :, :], ALU.add).then_inc(S["lg_w"], 1)
            dve.wait_ge(S["ld_be"], 16)

            def bias(ep, u, t, first=False):
                J = 8 * ep + 4 * u + t
                dve.wait_ge(S["f_mm"], J + 1)
                if not (first and u == 0 and t < 2):
                    dve.wait_ge(S["relu_done"], J - 1)
                dve.tensor_tensor(zb[t % 2], fbank[t], be_s[:, 2 * ep + u, :], ALU.add).then_inc(S["z_done"], 1)

            def gather(J, t):
                dve.wait_ge(S["relu_done"], J + 1)
                dve.tensor_tensor(x1[:, t, :], x1[:, t, :], rb[t % 2], ALU.add).then_inc(S["acc_done"], 1)

            for u in range(2):
                for t in range(TT):
                    bias(0, u, t, first=True)
                    if u or t:
                        if 4 * u + t > 4:
                            dve.wait_ge(S["acc_done"], 4 * u + t - 4)
                        gather(4 * u + t - 1, (t - 1) % 4)
            with dve.Fori(1, NE // 2) as ep:
                for u in range(2):
                    for t in range(TT):
                        bias(ep, u, t)
                        J = 8 * ep + 4 * u + t
                        dve.wait_ge(S["acc_done"], J - 4)
                        gather(J - 1, (t - 1) % 4)
            gather(4 * NE - 1, 3)
            dve.wait_ge(S["acc_done"], 4 * NE)
            norm(2)

        @block.tensor
        def _(pe):
            pe.wait_ge(S["ld_wx"], 16)
            for c in range(HC):
                pe.wait_ge(x_ld[c], 16)
                last = pe.matmul(PS[1][0:48, 512:1024], wx_s[:, c, :], xT_s[:, c, :], start=(c == 0), stop=(c == HC - 1))
            last.then_inc(S["xp_mm"], 1)
            pe.wait_ge(S["xp_sb"], 1)
            pe.wait_ge(S["ld_small"], 16 * N_SMALL)
            for b in range(NB):
                for c in range(HC):
                    pe.matmul(dtp[b][c], wdt_s[0:DTR, c * P:(c + 1) * P], xp_s[0:DTR, b * SX:(b + 1) * SX],
                              start=True, stop=True).then_inc(S["dtl_mm"], 1)
            pe.wait_ge(S["const_ready"], 2)

            PASS = ((0, 0), (0, 1), (1, 0))

            def kv_block(j, blk, src, w0):
                if blk < 2:
                    pe.wait_ge(S["k_n"], 2 * j + blk + 1)
                else:
                    pe.wait_ge(S["v_lo"], 2 * j + blk - 1)
                m = 0
                for a, w in PASS:
                    for c in range(HC):
                        last = pe.matmul(kvp[blk], src(a, c), pc[w][:, w0 + c, :], start=(m == 0), stop=(m == 11))
                        m += 1
                last.then_inc(S["kv_mm"], 1)

            def k_transpose(j, blk):
                pe.wait_ge(S["k_n"], 2 * j + blk + 3)
                pe.wait_ge(S["k_lo"], 2 * j + blk + 1)
                for h in range(4):
                    last = pe.transpose(ktp[blk][:, h * P:(h + 1) * P], kn[blk][:, h * P:(h + 1) * P], ident[:, :])
                last.then_inc(S["k_tr"], 1)

            def y_sum(b, i, pair):
                j = i + HC * b
                if pair == 0:
                    pe.wait_ge(S["xd_ready"], j + 1)
                    pe.wait_ge(S["r_ev"], j + 1)
                    for t in range(2):
                        pe.matmul(yp[:, t, :], xd[:, t * P:(t + 1) * P], ident[:, :], start=True, stop=False)
                pe.wait_ge(S["pair_added_p"] if pair else S["pair_added_v"], j + 1)
                for t in range(2):
                    for n in range(NPC):
                        at = n * SX + t * P
                        last = pe.matmul(yp[:, t, :], W[2 * pair + 1][:, at:at + P], ident[:, :], start=False,
                                         stop=(pair == 1 and n == NPC - 1))
                last.then_inc(S["y_mm"], 1)

            pe.sem_inc(S["v_lo"], 2)
            pe.sem_inc(S["k_lo"], 2)
            pe.sem_inc(S["k_tr"], 2)
            pe.sem_inc(S["k_n"], 2)
            pe.sem_inc(S["y_mm"], 2)
            pe.sem_inc(S["r_ev"], 1)
            for b in range(NB):
                with pe.Fori(0, HC) as i:
                    j = i + HC * b

                    def src(a, c):
                        return pc[a][:, PC_C[b] + j, c * P:(c + 1) * P]

                    def splits(groups):
                        pe.wait_ge(S["split_v"], 2 * groups)
                        pe.wait_ge(S["split_p"], 2 * groups)
                    splits((3, 6)[b])
                    kv_block(j, 0, src, PC_K)
                    kv_block(j, 1, src, PC_K + 4)
                    splits((5, 6)[b])
                    kv_block(j, 2, src, PC_V)
                    kv_block(j, 3, src, PC_V + 4)
                    k_transpose(j, 0)
                    k_transpose(j, 1)
                    y_sum(b, i, 0)
                    y_sum(b, i, 1)

            def xT_transpose(k):
                for c in range(HC):
                    for t in range(TT):
                        if c == 0:
                            pe.wait_ge(S["ln_x"], TT * k + t + 1)
                        last = pe.transpose(four[c][:, t * P:(t + 1) * P], x1[:, t, c * P:(c + 1) * P], ident[:, :])
                    last.then_inc(S["xT_tr"], 1)
            pe.wait_ge(S["r_ev"], NB * HC + 1)
            xT_transpose(0)
            pe.wait_ge(S["xT_lo"], HC)
            with pe.Fori(0, TT) as t:
                j = t + CT

                def srcx(a, c):
                    return xh[a][:, c, bass.ts(t, P)]
                kv_block(j, 0, srcx, PC_K)
                kv_block(j, 1, srcx, PC_K + 4)
                kv_block(j, 2, srcx, PC_V)
                kv_block(j, 3, srcx, PC_V + 4)
                k_transpose(j, 0)
                k_transpose(j, 1)

            def q_job(g, h, bank=PG):
                if h == 0:
                    pe.wait_ge(S["a_split"], g + 1)
                m = 0
                for w, a in PASS:
                    for c in range(HC):
                        last = pe.matmul(bank[:, :], wA[w][:, c, h * HD:(h + 1) * HD], xh[a][:, c, :],
                                         start=(m == 0), stop=(m == 11))
                        m += 1
                last.then_inc(S["q_mm"], 1)

            def ss_job(g, h, bank=PG):
                pe.wait_ge(S["q_sq"], 4 * g + h + 1)
                pe.wait_ge(S["q_lo"], 4 * g + h + 1)
                for t in range(TT):
                    last = pe.matmul(bank[:, t:t + 1], sqq[:, t * P:(t + 1) * P], ones[:, :], start=True, stop=True)
                last.then_inc(S["ss_mm"], 1)

            def wo_job(g, t):
                if t == 0:
                    pe.wait_ge(S["b_split"], g + 1)
                    pe.wait_ge(S["o_lo"], 4 * g + 4)
                m = 0
                for a, w in PASS:
                    for h in range(GRP):
                        last = pe.matmul(PG[:, :], oT[a][:, h, t * P:(t + 1) * P], wB[w][:, h, :],
                                         start=(m == 0), stop=(m == 11))
                        m += 1
                last.then_inc(S["wo_mm"], 1)

            def scores(g, s, n, first):
                h, t = s // 4, s % 4
                b = t // 2
                if not (first and s < 2):
                    pe.wait_ge(S["exp_done"], n - 1)
                if t == 0:
                    pe.wait_ge(S["q_lo"], 4 * g + h + 1)
                for m, (a, w) in enumerate(PASS):
                    pe.matmul(PS[s % 2][:, 0:SC], q[a][:, h, t * P:(t + 1) * P], kTc[w][:, g, b * SC:(b + 1) * SC],
                              start=(m == 0), stop=(m == 2))
                for m, (a, w) in enumerate(PASS):
                    last = pe.matmul(PS[s % 2][:, SC:KL], q[a][:, h, t * P:(t + 1) * P],
                                     kTx[w][:, g, b * KX:(b + 1) * KX], start=(m == 0), stop=(m == 2))
                last.then_inc(S["s_mm"], 1)

            def probs_T(s, n, first):
                pe.wait_ge(S["norm_done"], n - 1)
                if not (first and s < 3):
                    pe.wait_ge(S["pt_lo"], n - 2)
                for k in range(KT):
                    last = pe.transpose(PTT[:, k * P:(k + 1) * P], Pb[(s - 2) % 4][:, k * P:(k + 1) * P], ident[:, :])
                last.then_inc(S["t_done"], 1)

            def values(g, s, n, first):
                k4 = (s - 3) % SLOTS
                t = k4 % 4
                b = t // 2
                pe.wait_ge(S["pt_lo"], n - 2)
                if t == 0 and not (first and s == 3):
                    pe.wait_ge(S["o_lo"], 4 * g + k4 // 4)
                m = 0
                for w, a in PASS:
                    for k in range(KT):
                        v = Vc[w][:, b * 4 + k, bass.ts(g, HD)] if k < 4 else Vx[w][:, b * 2 + k - 4, bass.ts(g, HD)]
                        last = pe.matmul(PO[:, t * P:(t + 1) * P], v, pt[(s - 3) % 2][a][:, k, :],
                                         start=(m == 0), stop=(m == 3 * KT - 1))
                        m += 1
                last.then_inc(S["pv_done"], 1)

            def slot(g, s, first=False, final=False):
                n = SLOTS * g + s
                scores(g, s, n, first)
                if not (first and s < 2):
                    probs_T(s, n, first)
                if not (first and s < 3):
                    values(g if s >= 3 else g - 1, s, n, first)
                if s == 0:
                    ss_job(g, 3)
                if s in (3, 4, 5, 6) and not first:
                    if s == 3:
                        pe.wait_ge(S["ss_read"], 4 * g + 4)
                    else:
                        pe.wait_ge(S["wo_add"], 4 * g - 4 + s - 3)
                    wo_job(g - 1, s - 3)
                if not final:
                    if s in (9, 11, 13, 15):
                        h = (s - 9) // 2
                        if h == 0:
                            if first:
                                pe.wait_ge(S["ss_read"], 4)
                            else:
                                pe.wait_ge(S["wo_add"], 4 * g)
                        else:
                            pe.wait_ge(S["ss_read"], 4 * g + 4 + h)
                        q_job(g + 1, h)
                    if s in (10, 12, 14):
                        ss_job(g + 1, (s - 10) // 2)

            pe.wait_ge(S["k_lo"], 2 * (CT + TT) + 2)
            pe.wait_ge(S["v_lo"], 2 * (CT + TT) + 2)
            for h in range(GRP):
                q_job(0, h, q0b[h])
                if h:
                    ss_job(0, h - 1, q0b[h - 1])
            for s in range(SLOTS):
                slot(0, s, first=True)
            with pe.Fori(1, KVH - 1) as g:
                for s in range(SLOTS):
                    slot(g, s)
            for s in range(SLOTS):
                slot(KVH - 1, s, final=True)
            for s in range(3):
                n = SLOTS * KVH + s
                if s < 2:
                    probs_T(s, n, False)
                values(KVH - 1, s, n, False)
            for t in range(TT):
                pe.wait_ge(S["wo_add"], 4 * (KVH - 1) + t)
                wo_job(KVH - 1, t)
            xT_transpose(1)
            pe.wait_ge(S["xT_f"], HC)
            for t in range(TT):
                for c in range(HC):
                    last = pe.matmul(fbank[0][:, t * NE:(t + 1) * NE], x2T[:, c, t * P:(t + 1) * P], wg_s[:, c, :],
                                     start=(c == 0), stop=(c == HC - 1))
                last.then_inc(S["lg_mm"], 1)
            pe.wait_ge(S["lg_b"], TT)
            pe.wait_ge(S["xT_lo"], 2 * HC)

            def expert(ep, u, first=False):
                pe.wait_ge(S[("a_split", "b_split")[u]], KVH + 1 + ep)
                w = (wA, wB)[u]
                for t in range(TT):
                    if not (first and u == 0):
                        pe.wait_ge(S["z_done"], 8 * ep + 4 * u + t - 3)
                    m = 0
                    for a, l in PASS:
                        for c in range(HC):
                            last = pe.matmul(fbank[t], xh[a][:, c, t * P:(t + 1) * P], w[l][:, c, :],
                                             start=(m == 0), stop=(m == 11))
                            m += 1
                    last.then_inc(S["f_mm"], 1)
            expert(0, 0, first=True)
            expert(0, 1)
            with pe.Fori(1, NE // 2) as ep:
                expert(ep, 0)
                expert(ep, 1)


def flat(a):
    return a.rearrange("p c t -> p (c t)")


def kernel(x, ctx_4096, L0_attn_A_log, L0_attn_D, L0_attn_x_proj_w, L0_attn_dt_proj_w, L0_attn_dt_proj_b,
           L0_xattn_Wq, L0_xattn_Wk, L0_xattn_Wv, L0_xattn_Wo, L0_xattn_q_norm_w, L0_xattn_k_norm_w,
           L0_ffn_W_gate, L0_ffn_b_gate, L0_ffn_W_e, L0_ffn_b_e):
    import numpy as np
    import concourse.bacc as bacc
    from concourse.bass_utils import run_bass_kernel_spmd

    def a(v):
        return np.asarray(v)

    def chunked(w, cols):
        w = a(w)
        return w.reshape(HC, P, -1, cols).transpose(2, 1, 0, 3)

    wk, wv = chunked(L0_xattn_Wk, DM), chunked(L0_xattn_Wv, DM)
    ctx_t = a(ctx_4096).reshape(CT, P, HC, P).transpose(0, 3, 2, 1)
    ctx_t = ctx_t.reshape(CT, P, DM)
    pieces = np.concatenate([wk.transpose(0, 2, 1, 3).reshape(8, P, DM), ctx_t[:CT // 2],
                             wv.transpose(0, 2, 1, 3).reshape(8, P, DM), ctx_t[CT // 2:]])
    wq = chunked(L0_xattn_Wq, GRP * HD)
    wo = a(L0_xattn_Wo).reshape(KVH, GRP, HD, DM).transpose(0, 2, 1, 3)
    we = a(L0_ffn_W_e).reshape(NE, HC, P, DM).transpose(0, 2, 1, 3)
    arrays = {
        "xT": a(x).reshape(NT, DM).T,
        "pieces": pieces,
        "wx": a(L0_attn_x_proj_w).T,
        "wdt": a(L0_attn_dt_proj_w).T,
        "dtb": a(L0_attn_dt_proj_b).reshape(HC, P).T,
        "alog": a(L0_attn_A_log).reshape(HC, P, NS).transpose(1, 0, 2).reshape(P, HC * NS),
        "dskip": a(L0_attn_D).reshape(HC, P).T,
        "qnw": a(L0_xattn_q_norm_w).reshape(HD, 1),
        "knw": a(L0_xattn_k_norm_w).reshape(HD, 1),
        "wa": np.concatenate([wq, we[0::2]]),
        "wb": np.concatenate([wo, we[1::2]]),
        "wg": a(L0_ffn_W_gate),
        "bg": a(L0_ffn_b_gate),
        "be": a(L0_ffn_b_e),
    }
    nc = bacc.Bacc("TRN2", target_bir_lowering=False, num_devices=1)
    arrays = {k: np.ascontiguousarray(v) for k, v in arrays.items()}
    args = {k: nc.dram_tensor(k, v.shape, mybir.dt.from_np(v.dtype), kind="ExternalInput").ap() for k, v in arrays.items()}
    args["scratch"] = nc.dram_tensor("scratch", (2 * NS, NT), fp32).ap()
    args["out"] = nc.dram_tensor("out", (TT, P, DM), fp32, kind="ExternalOutput").ap()
    decoder_layer(nc, **args)
    r = run_bass_kernel_spmd(nc, [arrays], core_ids=[0])
    return np.asarray(r.results[0]["out"]).reshape(NB, SX, DM)
```

```python
import concourse.bass as bass
from concourse import mybir
from contextlib import ExitStack

fp32 = mybir.dt.float32
fp16 = mybir.dt.float16
u32 = mybir.dt.uint32
ALU = mybir.AluOpType
ACT = mybir.ActivationFunctionType
AX = mybir.AxisListType

P = 128
NB, SX, SC, DM = 2, 256, 512, 512
NT = NB * SX
TT = NT // P
CT = NB * SC // P
HC = DM // P
NS, DTR = 16, 16
NCH = 4
NPC = NS // NCH
KVH, HD, GRP = 8, 128, 4
KX = SX
KL = SC + SX
KT = KL // P
SLOTS = GRP * TT
WO_AT = (3, 4, 5, 6)
Q_AT = (11, 13, 15, 1)
SS_AT = (12, 14, 0, 7)
A_AT, B_AT = (3, 4, 6, 8), (10, 11, 13, 15)
NE = 8
RMS_EPS, LN_EPS = 1e-6, 1e-5
PIECES = 8 + CT + 8
PC_K, PC_V = 0, 12
PC_C = (8, 16)
SLOT_LD = 4


def decoder_layer(nc, xT, pieces, wx, wdt, dtb, alog, dskip, qnw, knw, wa, wb,
                  wg, bg, be, scratch, out):
    ctx = ExitStack()
    with ctx:
        def sb(name, shape, dt=fp32):
            return ctx.enter_context(nc.sbuf_tensor(name, shape, dt))

        def sem(name):
            return ctx.enter_context(nc.semaphore(name))

        class Arena:
            def __init__(self, name, kbytes):
                self.t, self.at, self.size = sb(name, [P, kbytes * 256]), 0, kbytes * 256

            def view(self, words, dt=fp32):
                v = self.t[:, self.at:self.at + words]
                self.at += words
                assert self.at <= self.size, (self.at, self.size)
                return v if dt == fp32 else v.bitcast(dt)

            def again(self):
                self.at = 0

        kTc = [sb(f"kTc_{s}", [P, KVH, NB * SC], fp16) for s in ("hi", "lo")]
        Vc = [sb(f"Vc_{s}", [P, CT, KVH * HD], fp16) for s in ("hi", "lo")]
        x1 = sb("x1", [P, TT, DM])
        ident = sb("ident", [P, P])
        ones = sb("ones", [P, 1])
        half = sb("half", [P, 8])
        dtb_s = sb("dtb_s", [P, HC])
        dsk_s = sb("dsk_s", [P, HC])
        A_s = sb("A_s", [P, HC * NS])
        qkw = sb("qkw", [P, 1])
        knw_s = sb("knw_s", [P, 1])
        xd = sb("xd", [P, SX])
        ssk = sb("ssk", [P, KVH])
        rk = sb("rk", [P, KVH])
        lnst = sb("lnst", [P, TT, 6])
        mv = sb("mv", [P, TT, 2])
        rstd = sb("rstd", [P, TT])
        mx = sb("mx", [P, SLOTS])
        negb = sb("negb", [P, SLOTS])
        lsum = sb("lsum", [P, SLOTS])
        rl = sb("rl", [P, SLOTS])
        ssq = sb("ssq", [P, GRP, TT])
        cq = sb("cq", [P, GRP, TT])
        wg_s = sb("wg_s", [P, HC, NE])
        bg_s = sb("bg_s", [P, NE])
        iot = sb("iot", [P, NE])
        RA = Arena("RA", 48)
        pc = [RA.view(PIECES * 256, fp16).rearrange("p (k n) -> p k n", k=PIECES) for _ in range(2)]
        RA.again()
        q = [RA.view(GRP * NT // 2, fp16).rearrange("p (h n) -> p h n", h=GRP) for _ in range(2)]
        sqq = RA.view(NT)
        pt = [[RA.view(KL // 2, fp16).rearrange("p (k n) -> p k n", k=KT) for _ in range(2)] for _ in range(2)]
        oT = [RA.view(GRP * NT // 2, fp16).rearrange("p (h n) -> p h n", h=GRP) for _ in range(2)]
        be_s = RA.view(NE * DM).rearrange("p (e n) -> p e n", e=NE)
        zb = [RA.view(DM) for _ in range(2)]
        rb = [RA.view(DM) for _ in range(2)]
        RB = Arena("RB", 84)
        Bb = RB.view(NS * SX).rearrange("p (n t) -> p n t", n=NS)
        Cb = RB.view(NS * SX).rearrange("p (n t) -> p n t", n=NS)
        xT_s = RB.view(HC * NT).rearrange("p (c t) -> p c t", c=HC)
        dA = [RB.view(NPC * SX) for _ in range(2)]
        W = [RB.view(NPC * SX) for _ in range(NCH)]
        stg = [RB.view(DM) for _ in range(SLOT_LD)]
        dt_s = RB.view(NB * HC * SX).rearrange("p (j t) -> p j t", j=NB * HC)
        kn = [RB.view(DM) for _ in range(2)]
        u_s = Vc[1][:, CT - 1, 0:512].bitcast(fp32)
        wdt_s, xp_s, wx_s = kn[0], kn[1], u_s[:, 0:HC * 48].rearrange("p (c r) -> p c r", c=HC)
        dA_all = RB.t[:, 2 * NS * SX + HC * NT:2 * NS * SX + HC * NT + 2 * NPC * SX]
        x1_all = x1[:, :, :].rearrange("p t n -> p (t n)")
        HW = HC * SX
        sp_e = [dA_all[:, 0:HW], x1_all[:, 0:HW]]
        sp_l = [dA_all[:, HW:2 * HW], x1_all[:, HW:2 * HW]]
        sp_r = [Vc[1][:, 2 + 2 * b:4 + 2 * b, :].rearrange("p k n -> p (k n)").bitcast(fp32) for b in range(NB)]
        sp_u = [Vc[0][:, 4 + 2 * b:6 + 2 * b, :].rearrange("p k n -> p (k n)").bitcast(fp32) for b in range(NB)]
        RB.again()
        kTx = [RB.view(KVH * NT // 2, fp16).rearrange("p (h n) -> p h n", h=KVH) for _ in range(2)]
        Vx = [RB.view(TT * 512, fp16).rearrange("p (k n) -> p k n", k=TT) for _ in range(2)]
        xh = [RB.view(HC * NT // 2, fp16).rearrange("p (c t) -> p c t", c=HC) for _ in range(2)]
        wA = [RB.view(HC * DM // 2, fp16).rearrange("p (c n) -> p c n", c=HC) for _ in range(2)]
        wA_f = RB.view(HC * DM).rearrange("p (c n) -> p c n", c=HC)
        wB = [RB.view(HC * DM // 2, fp16).rearrange("p (c n) -> p c n", c=HC) for _ in range(2)]
        wB_f = RB.view(HC * DM).rearrange("p (c n) -> p c n", c=HC)
        Pb_at = RB.at
        Pb = [RB.view(KL) for _ in range(4)]
        RB.at = Pb_at
        x2T = RB.view(HC * NT).rearrange("p (c t) -> p c t", c=HC)
        lgt, top, wsel, wtmp = (RB.view(TT * NE).rearrange("p (t e) -> p t e", t=TT) for _ in range(4))
        tix = RB.view(TT * NE, u32).rearrange("p (t e) -> p t e", t=TT)
        tixf = RB.view(TT * 2).rearrange("p (t e) -> p t e", t=TT)

        def pb(name, banks):
            return ctx.enter_context(nc.psum_tensor(name, [P, banks * 512], fp32))
        PS = [pb("PS0", 2), pb("PS1", 2)]
        PTT, PO, PG = pb("PTT", 2), pb("PO", 1), pb("PG", 1)
        kvp = [PS[0][:, 0:512], PS[0][:, 512:1024], PO[:, :], PG[:, :]]
        ktp = [PS[1][:, 0:512], PS[1][:, 512:1024]]
        yp = PTT[:, :].rearrange("p (t n) -> p t n", t=2)[:, :, 0:P]
        dtp = [[PTT[:, c * SX:(c + 1) * SX] for c in range(HC)],
               [PS[1][:, 512:768], PS[1][:, 768:1024], PG[:, 0:SX], PG[:, SX:2 * SX]]]
        ptb = [PTT[:, 0:512], PTT[:, 512:1024]]
        xtb = [kvp[0:2], ptb, ptb, [PO[:, :], PG[:, :]]]
        q0b = [PTT[:, 0:512], PTT[:, 512:1024], PO[:, :]]
        fbank = [PS[0][:, 0:512], PS[0][:, 512:1024], PS[1][:, 0:512], PS[1][:, 512:1024]]

        S = {n: sem(n) for n in (
            "ld_wx", "ld_small", "ld_be", "const_ready", "xp_mm", "xp_sb", "bc_out", "dtl_mm", "sp_abs",
            "sp_exp", "sp_ln", "sp_diff", "sp_max", "sp_inv", "sp_v", "A_exp", "A_ready", "qkw_ready", "dt_ready",
            "split_hi_v", "split_hi_a", "split_hi_p", "split_v", "split_p",
            "zero_ready", "xd_ready", "u_ready", "dA_ready", "dBx_ready", "h_ready", "g_ready",
            "pair_added_v", "pair_added_p", "y_mm", "r_ev",
             "kv_mm", "k_sq", "rk_tmp", "k_r", "k_n", "k_tr", "k_hi", "k_lo", "v_hi", "v_lo",
            "ln_st", "ln_mv", "ln_eps", "ln_rstd", "ln_x", "xT_tr", "xT_hi", "xT_lo", "xT_f",
            "a_ld", "a_hi", "a_split", "b_ld", "b_hi", "b_split",
            "s_mm", "mx_done", "negb_done", "exp_done", "rl_done", "norm_done", "t_done", "pt_hi", "pt_lo1", "pt_lo",
            "pv_done",
            "o_hi", "o_lo", "wo_mm", "wo_add", "q_mm", "q_hi", "q_sq", "q_lo", "ss_mm", "ss_read", "cq_done",
            "lg_mm", "lg_b", "lg_top", "lg_ix", "lg_f", "lg_eq", "lg_w", "f_mm", "z_done", "relu_done", "acc_done",
            "o_dma", "pool_waited")}
        x_ld = [sem(f"x_ld{c}") for c in range(HC)]
        pc_ld = [sem(f"pc_ld{k}") for k in range(SLOT_LD)]
        bc_ld = [sem(f"bc_ld{c}") for c in range(NCH)]
        N_SMALL = 8
        block = ctx.enter_context(nc.Block())

        def bc_chunk(b, c):
            for dst, row in ((Bb, 0), (Cb, NS)):
                src = scratch[row + c * NPC:row + (c + 1) * NPC, b * SX:(b + 1) * SX]
                nc.sync.dma_start(dst[:, c * NPC:(c + 1) * NPC, :], src.partition_broadcast(P)).then_inc(bc_ld[c], 16)

        @block.sync
        def _(sp):
            for c in range(HC):
                sp.dma_start(xT_s[:, c, :], xT[c * P:(c + 1) * P, :]).then_inc(x_ld[c], 16)

            def piece(i, k):
                sp.dma_start(stg[k], pieces[i * SLOT_LD + k, :, :]).then_inc(pc_ld[k], 16)

            for k in range(SLOT_LD):
                piece(0, k)

            def refill(i):
                for k in range(SLOT_LD):
                    sp.wait_ge(S["split_v"] if k < 2 else S["split_p"], 2 * i - 1 + k % 2)
                    piece(i, k)
            refill(1)
            sp.wait_ge(S["xp_sb"], 1)
            sp.dma_start(scratch, xp_s[DTR:DTR + 2 * NS, :]).then_inc(S["bc_out"], 16)
            refill(2)
            sp.wait_ge(S["bc_out"], 16)
            bc_chunk(0, 0)
            bc_chunk(0, 1)
            refill(3)
            bc_chunk(0, 2)
            refill(4)
            bc_chunk(0, 3)
            refill(5)
            for c in range(NCH):
                sp.wait_ge(S["g_ready"], HC * NCH - NCH + c + 1)
                bc_chunk(1, c)
            sp.wait_ge(S["r_ev"], NB * HC + 1)
            sp.dma_start(wA_f, wa[0]).then_inc(S["a_ld"], 16)
            sp.dma_start(wB_f, wb[0]).then_inc(S["b_ld"], 16)
            sp.wait_ge(S["kv_mm"], 4 * (CT + TT))
            sp.dma_start(be_s, be.partition_broadcast(P)).then_inc(S["ld_be"], 16)
            with sp.Fori(1, KVH + NE // 2) as i:
                sp.wait_ge(S["a_split"], i)
                sp.dma_start(wA_f, wa[i]).then_inc(S["a_ld"], 16)
                sp.wait_ge(S["b_split"], i)
                sp.dma_start(wB_f, wb[i]).then_inc(S["b_ld"], 16)
            for t in range(TT):
                sp.wait_ge(S["ln_x"], 2 * TT + t + 1)
                sp.dma_start(out[t], x1[:, t, :]).then_inc(S["o_dma"], 16)
            sp.wait_ge(S["o_dma"], 16 * TT)

        @block.gpsimd
        def _(pool):
            pool.memset(ident[:, :], 0.0).then_inc(S["const_ready"], 1)
            pool.wait_ge(S["const_ready"], 1)
            pool.affine_select(out=ident[:, :], in_=ident[:, :], compare_op=ALU.not_equal, fill=1.0, base=0,
                               pattern=[[-1, P]], channel_multiplier=1).then_inc(S["const_ready"], 1)
            pool.memset(ones[:, :], 1.0).then_inc(S["const_ready"], 1)
            pool.memset(half[:, :], -0.5).then_inc(S["const_ready"], 1)
            for e in range(NE):
                pool.memset(iot[:, e:e + 1], float(e)).then_inc(S["const_ready"], 1)

            def waited():
                pool.sem_inc(S["pool_waited"], 1)

            def hi_lo(src, hi, lo, s_hi, n, s_lo):
                pool.tensor_scalar(hi, src, 1.0, 1.0, ALU.mult, ALU.mult).then_inc(s_hi, 1)
                pool.wait_ge(s_hi, n + 1)
                pool.tensor_tensor(lo, src, hi, ALU.subtract).then_inc(s_lo, 1)

            def split(i):
                for k in (2, 3):
                    pool.wait_ge(pc_ld[k], 16 * i + 16)
                    if i >= 3:
                        pool.wait_ge(S["split_hi_a"], SLOT_LD * (i - 3) + k + 1)
                        pool.tensor_tensor(pc[1][:, i * SLOT_LD + k, :], stg[k], pc[0][:, i * SLOT_LD + k, :],
                                           ALU.subtract).then_inc(S["split_p"], 1)
                        continue
                    hi_lo(stg[k], pc[0][:, i * SLOT_LD + k, :], pc[1][:, i * SLOT_LD + k, :],
                          S["split_hi_p"], 2 * i + k - 2, S["split_p"])

            def rk_of(j):
                pool.wait_ge(S["k_sq"], 2 * j + 2)
                waited()
                pool.tensor_scalar(rk[:, :], ssk[:, :], 1.0 / HD, RMS_EPS, ALU.mult, ALU.add).then_inc(S["rk_tmp"], 1)
                pool.wait_ge(S["rk_tmp"], j + 1)
                pool.tensor_tensor(rk[:, :], rk[:, :], half[:, :], ALU.pow).then_inc(S["k_r"], 1)

            def scan_step(b, i, first=False):
                j = i + HC * b
                pool.tensor_tensor(u_s, dt_s[:, j, :], xT_s[:, i, b * SX:(b + 1) * SX], ALU.mult)\
                    .then_inc(S["u_ready"], 1)
                for c in range(NCH):
                    pool.wait_ge(bc_ld[c], 32 * (b + 1))
                    if c == 0:
                        pool.wait_ge(S["u_ready"], j + 1)
                    if c % 2:
                        pool.wait_ge(S["y_mm"], 2 * j + c // 2 + 1)
                    elif not first:
                        pool.wait_ge(S["pair_added_v"] if c else S["pair_added_p"], j)
                    ub = u_s.unsqueeze(1).broadcast_to([P, NPC, SX])
                    pool.tensor_tensor(W[c].rearrange("p (n t) -> p n t", n=NPC), Bb[:, c * NPC:(c + 1) * NPC, :],
                                       ub, ALU.mult).then_inc(S["dBx_ready"], 1)
                    if first and c in (1, 2):
                        split(2 + c)
                pool.wait_ge(S["g_ready"], NCH * j + 2)
                pool.tensor_tensor(W[1], W[1], W[0], ALU.add).then_inc(S["pair_added_p"], 1)
                rk_of(j)

            def w_piece(s, i, c, free=None):
                if free:
                    pool.wait_ge(*free)
                f, w, ld, h, sp_ = ((wA_f, wA, "a_ld", "a_hi", "a_split"), (wB_f, wB, "b_ld", "b_hi", "b_split"))[s]
                if c == 0:
                    pool.wait_ge(S[ld], 16 * i + 16)
                    waited()
                pool.tensor_scalar(w[0][:, c, :], f[:, c, :], 1.0, 1.0, ALU.mult, ALU.mult).then_inc(S[h], 1)
                pool.wait_ge(S[h], 4 * i + c + 1)
                last = pool.tensor_tensor(w[1][:, c, :], f[:, c, :], w[0][:, c, :], ALU.subtract)
                if c == HC - 1:
                    last.then_inc(S[sp_], 1)

            def ln_rstd(m):
                h = 2 * (m % 2)
                pool.wait_ge(S["ln_mv"], 2 * (m + 1))
                pool.tensor_scalar(rstd[:, h:h + 2], mv[:, h:h + 2, 1], LN_EPS, 1.0, ALU.add, ALU.mult)\
                    .then_inc(S["ln_eps"], 1)
                pool.wait_ge(S["ln_eps"], m + 1)
                pool.tensor_tensor(rstd[:, h:h + 2], rstd[:, h:h + 2], half[:, 0:2], ALU.pow).then_inc(S["ln_rstd"], 1)

            for i in range(3):
                split(i)
            pool.wait_ge(S["dt_ready"], 1)
            scan_step(0, 0, first=True)
            with pool.Fori(1, HC - 1) as i:
                scan_step(0, i)
            split(5)
            scan_step(0, HC - 1)
            pool.wait_ge(S["dt_ready"], 2)
            with pool.Fori(0, HC - 1) as i:
                scan_step(1, i)
            ln_rstd(0)
            scan_step(1, HC - 1)
            ln_rstd(1)
            rk_of(CT)
            pool.wait_ge(S["y_mm"], 2 * NB * HC + 2)
            for c in range(HC):
                w_piece(0, 0, c)
            with pool.Fori(CT + 1, CT + TT) as j:
                rk_of(j)

            def cq_of(g, h):
                pool.wait_ge(S["ss_read"], 4 * g + h + 1)
                pool.tensor_tensor(cq[:, h, :], ssq[:, h, :], half[:, 0:TT], ALU.pow).then_inc(S["cq_done"], 1)

            for h in range(2):
                cq_of(0, h)

            def slot(g, s, first=False, last=False):
                n = SLOTS * g + s
                if not (first and s == 0):
                    pool.wait_ge(S["rl_done"], n)
                    k = (s - 1) % SLOTS
                    waited()
                    pool.tensor_scalar(Pb[(s - 1) % 4], Pb[(s - 1) % 4], rl[:, k:k + 1], 1.0, ALU.mult, ALU.mult)\
                        .then_inc(S["norm_done"], 1)
                if last:
                    return
                if s in SS_AT[2:]:
                    cq_of(g, SS_AT.index(s))
                if s in A_AT:
                    w_piece(0, g + 1, A_AT.index(s), (S["q_mm"], 4 * g + 4) if s == A_AT[0] else None)
                if s in B_AT:
                    w_piece(1, g, B_AT.index(s), (S["wo_mm"], 4 * g) if s == B_AT[0] and not first else None)

            def body(g, first=False, final=False):
                for s in range(SLOTS):
                    slot(g, s, first)
                    if not final and s in SS_AT[:2]:
                        cq_of(g + 1, SS_AT.index(s))

            body(0, first=True)
            with pool.Fori(1, KVH - 1) as g:
                body(g)
            body(KVH - 1, final=True)
            slot(KVH, 0, last=True)
            ln_rstd(2)
            ln_rstd(3)
            pool.wait_ge(S["wo_mm"], 4 * KVH)
            for c in range(HC):
                w_piece(1, KVH, c)
            with pool.Fori(1, NE // 2) as k:
                for c in range(HC):
                    w_piece(0, KVH + k, c, (S["f_mm"], 8 * k - 4) if c == 0 else None)
                for c in range(HC):
                    w_piece(1, KVH + k, c, (S["f_mm"], 8 * k) if c == 0 else None)
            ln_rstd(4)
            ln_rstd(5)

        @block.scalar
        def _(act):
            act.dma_start(wx_s, wx.rearrange("(c p) r -> p c r", p=P)).then_inc(S["ld_wx"], 16)
            small = [(wdt_s[0:DTR, :], wdt), (dtb_s[:, :], dtb),
                     (A_s[:, :], alog), (dsk_s[:, :], dskip), (qkw[:, :], qnw), (knw_s[:, :], knw),
                     (wg_s[:, :, :], wg.rearrange("(c p) e -> p c e", p=P)), (bg_s[:, :], bg.partition_broadcast(P))]
            assert len(small) == N_SMALL
            for dst, src in small:
                act.dma_start(dst, src).then_inc(S["ld_small"], 16)
            act.wait_ge(S["xp_mm"], 1)
            act.activation(xp_s[0:48, :], PS[1][0:48, 512:1024], ACT.Copy).then_inc(S["xp_sb"], 1)
            act.wait_ge(S["ld_small"], 16 * N_SMALL)
            act.activation(A_s[:, :], A_s[:, :], ACT.Exp).then_inc(S["A_exp"], 1)
            for b in range(NB):
                act.wait_ge(S["dtl_mm"], HC * (b + 1))
                for c in range(HC):
                    act.activation(dt_s[:, HC * b + c, :], dtp[b][c], ACT.Abs, bias=dtb_s[:, c:c + 1])\
                        .then_inc(S["sp_abs"], 1)
                act.wait_ge(S["sp_abs"], HC * (b + 1))
                act.activation(sp_e[b], flat(dt_s[:, HC * b:HC * b + HC, :]), ACT.Exp, scale=-1.0)\
                    .then_inc(S["sp_exp"], 1)
                act.wait_ge(S["sp_exp"], b + 1)
                act.activation(sp_l[b], sp_e[b], ACT.Ln, bias=1.0).then_inc(S["sp_ln"], 1)
                act.wait_ge(S["sp_ln"], b + 1)
                act.activation(sp_r[b], sp_l[b], ACT.Exp, scale=-1.0).then_inc(S["sp_inv"], 1)
            act.wait_ge(S["A_ready"], 1)
            act.wait_ge(S["zero_ready"], 2)

            def exps(j, i, c):
                act.wait_ge(S["h_ready"], NCH * j + c + 1)
                for n in range(NPC):
                    last = act.activation(dA[c % 2][:, n * SX + 1:(n + 1) * SX], dt_s[:, j, 1:SX],
                                          ACT.Exp, scale=A_s[:, bass.ds(i * NS + c * NPC + n, 1)])
                last.then_inc(S["dA_ready"], 1)

            def k_square(j, blk):
                act.wait_ge(S["kv_mm"], 4 * j + blk + 1)
                act.wait_ge(S["k_tr"], 2 * j + blk + 1)
                for h in range(4):
                    last = act.activation(kn[blk][:, h * HD:(h + 1) * HD], kvp[blk][:, h * HD:(h + 1) * HD], ACT.Square,
                                          accum_out=ssk[:, 4 * blk + h:4 * blk + h + 1])
                last.then_inc(S["k_sq"], 1)

            def k_high(j, blk, dst):
                act.wait_ge(S["k_tr"], 2 * j + blk + 3)
                act.activation(dst, ktp[blk].rearrange("p (h t) -> p h t", h=4), ACT.Copy, scale=qkw[:, 0:1])\
                    .then_inc(S["k_hi"], 1)

            def v_high(j, blk, dst):
                act.wait_ge(S["kv_mm"], 4 * j + 2 + blk + 1)
                act.activation(dst, kvp[2 + blk], ACT.Copy).then_inc(S["v_hi"], 1)

            act.wait_ge(S["qkw_ready"], 2)
            act.wait_ge(S["dt_ready"], 1)

            def y_evac(b, i):
                act.wait_ge(S["y_mm"], 2 * (i + HC * b) + 4)
                act.wait_ge(S["dt_ready"], 2)
                act.activation(x1[:, 2 * b:2 * b + 2, bass.ts(i, P)], yp, ACT.Copy).then_inc(S["r_ev"], 1)

            def split_high(i):
                for k in range(SLOT_LD):
                    act.wait_ge(pc_ld[k], 16 * i + 16)
                    act.activation(pc[0][:, i * SLOT_LD + k, :], stg[k], ACT.Copy).then_inc(S["split_hi_a"], 1)

            def ctx_k_high(b, i):
                j = i + HC * b
                for k in range(2):
                    k_high(j, k, kTc[0][:, 4 * k:4 * k + 4, bass.ts(j, P)])

            def scan_step(b, i, former):
                j = i + HC * b
                vd = [Vc[0][:, j, 512 * k:512 * k + 512] for k in range(2)]
                exps(j, i, 0)
                exps(j, i, 1)
                if not former:
                    split_high(3)
                    for c in range(HC):
                        act.activation(dt_s[:, HC + c, :], dtp[1][c], ACT.Relu, bias=dtb_s[:, c:c + 1])\
                            .then_inc(S["sp_max"], 1)
                if former:
                    y_evac(*former)
                    ctx_k_high(*former)
                act.activation(xd[:, :], xT_s[:, i, b * SX:(b + 1) * SX], ACT.Copy, scale=dsk_s[:, bass.ds(i, 1)])\
                    .then_inc(S["xd_ready"], 1)
                k_square(j, 0)
                exps(j, i, 2)
                k_square(j, 1)
                if not former:
                    split_high(4)
                exps(j, i, 3)
                if not former:
                    split_high(5)
                v_high(j, 0, vd[0])
                v_high(j, 1, vd[1])

            scan_step(0, 0, None)
            with act.Fori(1, HC) as i:
                scan_step(0, i, (0, i - 1))
            act.wait_ge(S["dt_ready"], 2)
            scan_step(1, 0, (0, HC - 1))
            with act.Fori(1, HC) as i:
                scan_step(1, i, (1, i - 1))
            y_evac(1, HC - 1)
            ctx_k_high(1, HC - 1)

            def xT_high(m, wide):
                for c in range(2):
                    bank = xtb[m][c].rearrange("p (c t) -> p c t", c=2)
                    part = (slice(None), slice(2 * c, 2 * c + 2), slice(m % 2 * SX, (m % 2 + 1) * SX))
                    act.wait_ge(S["xT_tr"], 2 * m + c + 1)
                    act.activation(xh[0][part], bank, ACT.Copy).then_inc(S["xT_hi"], 1)
                for c in range(2 * wide):
                    bank = xtb[m][c].rearrange("p (c t) -> p c t", c=2)
                    act.wait_ge(S["xT_lo"], 2 * m + c + 1)
                    act.activation(x2T[:, 2 * c:2 * c + 2, m % 2 * SX:(m % 2 + 1) * SX], bank, ACT.Copy)\
                        .then_inc(S["xT_f"], 1)

            def kv_high(t, squared=False):
                j = t + CT
                if not squared:
                    for blk in range(2):
                        k_square(j, blk)
                for blk in range(2):
                    v_high(j, blk, Vx[0][:, t, 512 * blk:512 * blk + 512])
                    k_high(j, blk, kTx[0][:, 4 * blk:4 * blk + 4, bass.ts(t, P)])

            xT_high(0, False)
            for blk in range(2):
                k_square(CT, blk)
            xT_high(1, False)
            kv_high(0, squared=True)
            with act.Fori(1, TT) as t:
                kv_high(t)

            def q_evac(g, h, bank=PG, first=False):
                n = 4 * g + h
                act.wait_ge(S["q_mm"], n + 1)
                act.activation(q[0][:, h, :], bank[:, :], ACT.Copy).then_inc(S["q_hi"], 1)
                if not (first and h == 0):
                    act.wait_ge(S["ss_mm"], n)
                act.activation(sqq, bank[:, :], ACT.Square).then_inc(S["q_sq"], 1)

            def slot(g, s, first=False, final=False):
                n = SLOTS * g + s
                if not (first and s < 2):
                    act.wait_ge(S["t_done"], n - 1)
                    if not (first and s < 4):
                        act.wait_ge(S["pv_done"], n - 3)
                    act.activation(pt[s % 2][0], PTT[:, 0:KL].rearrange("p (k n) -> p k n", k=KT), ACT.Copy)\
                        .then_inc(S["pt_hi"], 1)
                act.wait_ge(S["negb_done"], n + 1)
                if not (first and s < 4):
                    act.wait_ge(S["t_done"], n - 3)
                h, t = s // 4, s % 4
                act.activation(Pb[s % 4], PS[s % 2][:, 0:KL], ACT.Exp, scale=cq[:, h, t:t + 1],
                               bias=negb[:, s:s + 1], accum_out=lsum[:, s:s + 1]).then_inc(S["exp_done"], 1)
                if s % 4 == 2 and not (first and s == 2):
                    h = (s // 4 - 1) % 4
                    act.wait_ge(S["pv_done"], n - 2)
                    if s > 2 and not first:
                        act.wait_ge(S["wo_mm"], 4 * g)
                    act.activation(oT[0][:, h, :], PO[:, :], ACT.Copy).then_inc(S["o_hi"], 1)
                if s == Q_AT[3]:
                    q_evac(g, 3)
                if s in Q_AT[:3] and not final:
                    q_evac(g + 1, Q_AT.index(s))

            act.wait_ge(S["kv_mm"], 4 * (CT + TT))
            for h in range(GRP - 1):
                q_evac(0, h, q0b[h], first=True)
            for s in range(SLOTS):
                slot(0, s, first=True)
            with act.Fori(1, KVH - 1) as g:
                for s in range(SLOTS):
                    slot(g, s)
            for s in range(SLOTS):
                slot(KVH - 1, s, final=True)
            for s in range(2):
                n = SLOTS * KVH + s
                act.wait_ge(S["t_done"], n - 1)
                act.wait_ge(S["pv_done"], n - 3)
                act.activation(pt[s % 2][0], PTT[:, 0:KL].rearrange("p (k n) -> p k n", k=KT), ACT.Copy)\
                    .then_inc(S["pt_hi"], 1)
                act.wait_ge(S["pv_done"], SLOTS * KVH - 2 + 2 * s)
                act.activation(oT[0][:, 3, s * SX:(s + 1) * SX], PO[:, s * SX:(s + 1) * SX], ACT.Copy)\
                    .then_inc(S["o_hi"], 1)
            xT_high(2, True)
            xT_high(3, True)

            def relu(ep, u, t, first=False):
                J = 8 * ep + 4 * u + t
                act.wait_ge(S["z_done"], J + 1)
                if not (first and u == 0 and t < 2):
                    act.wait_ge(S["acc_done"], J - 1)
                act.activation(rb[t % 2], zb[t % 2], ACT.Relu, scale=wsel[:, t, bass.ds(2 * ep + u, 1)])\
                    .then_inc(S["relu_done"], 1)

            act.wait_ge(S["lg_w"], 1)
            for u in range(2):
                for t in range(TT):
                    relu(0, u, t, first=True)
            with act.Fori(1, NE // 2) as ep:
                for u in range(2):
                    for t in range(TT):
                        relu(ep, u, t)

        @block.vector
        def _(dve):
            def split(i, k):
                dve.wait_ge(pc_ld[k], 16 * i + 16)
                if i < 3:
                    dve.tensor_copy(pc[0][:, i * SLOT_LD + k, :], stg[k]).then_inc(S["split_hi_v"], 1)
                    dve.wait_ge(S["split_hi_v"], 2 * i + k + 1)
                else:
                    dve.wait_ge(S["split_hi_a"], SLOT_LD * (i - 3) + k + 1)
                dve.tensor_tensor(pc[1][:, i * SLOT_LD + k, :], stg[k], pc[0][:, i * SLOT_LD + k, :], ALU.subtract)\
                    .then_inc(S["split_v"], 1)

            dve.wait_ge(S["ld_small"], 16 * N_SMALL)
            dve.tensor_tensor(qkw[:, :], qkw[:, :], knw_s[:, :], ALU.mult).then_inc(S["qkw_ready"], 1)
            dve.tensor_scalar(dsk_s[:, :], dsk_s[:, :], 1.0, None, ALU.add).then_inc(S["qkw_ready"], 1)
            def splits(i):
                split(i, 0)
                split(i, 1)

            splits(0)
            splits(1)
            dve.wait_ge(S["A_exp"], 1)
            dve.tensor_scalar(A_s[:, :], A_s[:, :], -1.0, None, ALU.mult).then_inc(S["A_ready"], 1)

            def sp_error(b):
                dve.wait_ge(S["sp_exp"], b + 1)
                dve.tensor_scalar(sp_u[b], sp_e[b], 1.0, None, ALU.add).then_inc(S["sp_v"], 1)
                dve.wait_ge(S["sp_v"], 3 * b + 1)
                dve.scalar_tensor_tensor(sp_u[b], sp_u[b], -1.0, sp_e[b], ALU.add, ALU.subtract)\
                    .then_inc(S["sp_diff"], 1)

            def sp_positive(b):
                for c in range(HC):
                    dve.tensor_scalar(dt_s[:, HC * b + c, :], dtp[b][c], dtb_s[:, c:c + 1], 0.0, ALU.add, ALU.max)\
                        .then_inc(S["sp_max"], 1)

            def sp_sum(b):
                r, l, u = sp_r[b], sp_l[b], sp_u[b]
                d = flat(dt_s[:, HC * b:HC * b + HC, :])
                dve.wait_ge(S["sp_diff"], b + 1)
                dve.wait_ge(S["sp_inv"], b + 1)
                dve.tensor_tensor(u, u, r, ALU.mult).then_inc(S["sp_v"], 1)
                dve.wait_ge(S["sp_v"], 3 * b + 2)
                dve.tensor_tensor(l, l, u, ALU.subtract).then_inc(S["sp_v"], 1)
                dve.wait_ge(S["sp_v"], 3 * b + 3)
                dve.wait_ge(S["sp_max"], HC * (b + 1))
                dve.tensor_tensor(d, d, l, ALU.add).then_inc(S["dt_ready"], 1)

            sp_error(0)
            dve.wait_ge(S["sp_exp"], 1)
            sp_positive(0)
            sp_sum(0)
            dve.wait_ge(S["dt_ready"], 1)
            for k in range(2):
                z = dA[k].rearrange("p (n t) -> p n t", n=NPC)[:, :, 0:1]
                dve.memset(z, 0.0).then_inc(S["zero_ready"], 1)
            dve.sem_inc(S["h_ready"], 2)
            splits(2)
            sp_error(1)

            def k_norm(j, blk):
                dve.wait_ge(S["k_r"], j + 1)
                r = rk[:, 4 * blk:4 * blk + 4].unsqueeze(2).broadcast_to([P, 4, HD])
                dve.tensor_tensor(kn[blk].rearrange("p (h d) -> p h d", h=4),
                                  kvp[blk].rearrange("p (h d) -> p h d", h=4), r, ALU.mult).then_inc(S["k_n"], 1)

            def k_low(j, blk, hi, lo):
                dve.wait_ge(S["k_hi"], 2 * j + blk + 1)
                dve.scalar_tensor_tensor(lo, ktp[blk].rearrange("p (h t) -> p h t", h=4), qkw[:, 0:1], hi,
                                         ALU.mult, ALU.subtract).then_inc(S["k_lo"], 1)

            def v_low(j, blk, hi, lo):
                dve.wait_ge(S["v_hi"], 2 * j + blk + 1)
                dve.tensor_tensor(lo, kvp[2 + blk], hi, ALU.subtract).then_inc(S["v_lo"], 1)

            def ctx_k_low(b, i, blk):
                j = i + HC * b
                k_low(j, blk, *[kTc[w][:, 4 * blk:4 * blk + 4, bass.ts(j, P)] for w in range(2)])

            def scan_step(b, i, former):
                j = i + HC * b
                vd = [[Vc[w][:, j, 512 * k:512 * k + 512] for w in range(2)] for k in range(2)]

                def scan(c):
                    dve.wait_ge(S["dA_ready"], NCH * j + c + 1)
                    dve.wait_ge(S["dBx_ready"], NCH * j + c + 1)
                    dve.tensor_tensor_scan(W[c], dA[c % 2], W[c], 0.0, ALU.mult, ALU.add).then_inc(S["h_ready"], 1)
                    dve.wait_ge(S["h_ready"], NCH * j + c + 3)
                    dve.tensor_tensor(W[c], W[c], Cb[:, c * NPC:(c + 1) * NPC, :].rearrange("p n t -> p (n t)"),
                                      ALU.mult).then_inc(S["g_ready"], 1)

                scan(0)
                if not former:
                    splits(3)
                scan(1)
                if former:
                    ctx_k_low(*former, 0)
                else:
                    sp_sum(1)
                scan(2)
                if former:
                    ctx_k_low(*former, 1)
                else:
                    splits(4)
                scan(3)
                dve.wait_ge(S["g_ready"], NCH * j + NCH)
                dve.tensor_tensor(W[3], W[3], W[2], ALU.add).then_inc(S["pair_added_v"], 1)
                k_norm(j, 0)
                k_norm(j, 1)
                v_low(j, 0, *vd[0])
                v_low(j, 1, *vd[1])

            scan_step(0, 0, None)
            with dve.Fori(1, HC - 1) as i:
                scan_step(0, i, (0, i - 1))
            splits(5)
            scan_step(0, HC - 1, (0, HC - 2))

            def stats(m, tiles=(0, 1), end=True):
                for t in tiles:
                    dve.bn_stats(lnst[:, m % 2 * 2 + t, :], x1[:, m % 2 * 2 + t, :]).then_inc(S["ln_st"], 1)
                for t in range(2 * end):
                    dve.wait_ge(S["ln_st"], 2 * m + t + 1)
                    dve.bn_aggr(mv[:, m % 2 * 2 + t, :], lnst[:, m % 2 * 2 + t, :]).then_inc(S["ln_mv"], 1)

            def apply_norm(m):
                dve.wait_ge(S["ln_mv"], 2 * m + 2)
                dve.wait_ge(S["ln_rstd"], m + 1)
                for t in range(m % 2 * 2, m % 2 * 2 + 2):
                    dve.tensor_scalar(x1[:, t, :], x1[:, t, :], mv[:, t, 0:1], rstd[:, t:t + 1],
                                      ALU.subtract, ALU.mult).then_inc(S["ln_x"], 1)

            def xT_low(m):
                for c in range(2):
                    bank = xtb[m][c].rearrange("p (c t) -> p c t", c=2)
                    part = (slice(None), slice(2 * c, 2 * c + 2), slice(m % 2 * SX, (m % 2 + 1) * SX))
                    dve.wait_ge(S["xT_hi"], 2 * m + c + 1)
                    dve.tensor_tensor(xh[1][part], bank, xh[0][part], ALU.subtract).then_inc(S["xT_lo"], 1)

            def kv_low(t):
                j = t + CT
                k_norm(j, 0)
                k_norm(j, 1)
                for blk in range(2):
                    v_low(j, blk, *[Vx[w][:, t, 512 * blk:512 * blk + 512] for w in range(2)])
                    k_low(j, blk, *[kTx[w][:, 4 * blk:4 * blk + 4, bass.ts(t, P)] for w in range(2)])

            scan_step(1, 0, (0, HC - 1))
            dve.wait_ge(S["r_ev"], HC + 1)
            stats(0)
            with dve.Fori(1, HC - 1) as i:
                scan_step(1, i, (1, i - 1))
            apply_norm(0)
            scan_step(1, HC - 1, (1, HC - 2))
            ctx_k_low(1, HC - 1, 0)
            ctx_k_low(1, HC - 1, 1)
            xT_low(0)
            dve.wait_ge(S["r_ev"], NB * HC + 1)
            stats(1)
            apply_norm(1)
            xT_low(1)
            kv_low(0)
            with dve.Fori(1, TT) as t:
                kv_low(t)

            def q_low(g, h, bank=PG):
                dve.wait_ge(S["q_hi"], 4 * g + h + 1)
                dve.wait_ge(S["q_sq"], 4 * g + h + 1)
                dve.tensor_tensor(q[1][:, h, :], bank[:, :], q[0][:, h, :], ALU.subtract).then_inc(S["q_lo"], 1)

            def ss_evac(g, h, bank=PG):
                dve.wait_ge(S["ss_mm"], 4 * g + h + 1)
                dve.tensor_scalar(ssq[:, h, :], bank[:, 0:TT], HD * RMS_EPS, None, ALU.add).then_inc(S["ss_read"], 1)

            def pt_low(n, s):
                dve.wait_ge(S["pt_hi"], n - 1)
                for done, k0, k1 in (("pt_lo1", 0, 4), ("pt_lo", 4, KT)):
                    dve.tensor_tensor(pt[s % 2][1][:, k0:k1, :], PTT[:, k0 * P:k1 * P].rearrange("p (k n) -> p k n", n=P),
                                      pt[s % 2][0][:, k0:k1, :], ALU.subtract).then_inc(S[done], 1)

            def o_low(n, h):
                dve.wait_ge(S["o_hi"], n)
                dve.tensor_tensor(oT[1][:, h, :], PO[:, :], oT[0][:, h, :], ALU.subtract).then_inc(S["o_lo"], 1)

            def wo_add(g, t, bank=PG):
                dve.wait_ge(S["wo_mm"], 4 * g + t + 1)
                dve.tensor_tensor(x1[:, t, :], x1[:, t, :], bank[:, :], ALU.add).then_inc(S["wo_add"], 1)

            def recip(n, s):
                dve.wait_ge(S["exp_done"], n)
                k = (s - 1) % SLOTS
                dve.reciprocal(rl[:, k:k + 1], lsum[:, k:k + 1]).then_inc(S["rl_done"], 1)

            def slot(g, s, first=False, final=False):
                n = SLOTS * g + s
                if not (first and s == 0):
                    recip(n, s)
                dve.wait_ge(S["s_mm"], n + 1)
                dve.reduce_max(mx[:, s:s + 1], PS[s % 2][:, 0:KL], AX.X).then_inc(S["mx_done"], 1)
                if s % 4 == 0:
                    dve.wait_ge(S["cq_done"], 4 * g + s // 4 + 1)
                dve.wait_ge(S["mx_done"], n + 1)
                dve.scalar_tensor_tensor(negb[:, s:s + 1], mx[:, s:s + 1], -1.0, cq[:, s // 4, s % 4:s % 4 + 1],
                                         ALU.mult, ALU.mult).then_inc(S["negb_done"], 1)
                if not (first and s < 2):
                    pt_low(n, s)
                if s in WO_AT and not first:
                    wo_add(g - 1, WO_AT.index(s))
                if s in SS_AT[2:]:
                    ss_evac(g, SS_AT.index(s))
                if s in SS_AT[:2] and not final:
                    ss_evac(g + 1, SS_AT.index(s))
                if s % 4 == 2 and not (first and s == 2):
                    o_low(4 * g + s // 4, (s // 4 - 1) % 4)
                if s == Q_AT[3]:
                    q_low(g, 3)
                if s in Q_AT[:3] and not final:
                    q_low(g + 1, Q_AT.index(s))

            dve.wait_ge(S["kv_mm"], 4 * (CT + TT))
            for h in range(GRP - 1):
                q_low(0, h, q0b[h])
                if h:
                    ss_evac(0, h - 1, q0b[h - 1])
            for s in range(SLOTS):
                slot(0, s, first=True)
            with dve.Fori(1, KVH - 1) as g:
                for s in range(SLOTS):
                    slot(g, s)
            for s in range(SLOTS):
                slot(KVH - 1, s, final=True)
            recip(SLOTS * KVH, 0)

            def o_low_half(b):
                part = slice(b * SX, (b + 1) * SX)
                dve.wait_ge(S["o_hi"], 4 * KVH + b)
                dve.tensor_tensor(oT[1][:, 3, part], PO[:, part], oT[0][:, 3, part], ALU.subtract).then_inc(S["o_lo"], 1)

            pt_low(SLOTS * KVH, 0)
            o_low_half(0)
            wo_add(KVH - 1, 0, fbank[0])
            wo_add(KVH - 1, 1, fbank[1])
            dve.wait_ge(S["wo_add"], 4 * KVH - 2)
            stats(2)
            pt_low(SLOTS * KVH + 1, 1)
            apply_norm(2)
            o_low_half(1)
            xT_low(2)
            wo_add(KVH - 1, 2, fbank[2])
            wo_add(KVH - 1, 3, fbank[3])
            dve.wait_ge(S["wo_add"], 4 * KVH)
            stats(3)
            apply_norm(3)
            xT_low(3)
            dve.wait_ge(S["const_ready"], 4 + NE)
            for t in range(TT):
                dve.wait_ge(S["lg_mm"], TT)
                dve.tensor_tensor(lgt[:, t, :], PTT[:, t * NE:(t + 1) * NE], bg_s[:, :], ALU.add)\
                    .then_inc(S["lg_b"], 1)
            for t in range(TT):
                dve.wait_ge(S["lg_b"], t + 1)
                dve.max(top[:, t, :], lgt[:, t, :]).then_inc(S["lg_top"], 1)
            for t in range(TT):
                dve.wait_ge(S["lg_top"], t + 1)
                dve.max_index(tix[:, t, :], top[:, t, :], lgt[:, t, :]).then_inc(S["lg_ix"], 1)
            dve.wait_ge(S["lg_ix"], TT)
            dve.tensor_copy(tixf[:, :, :], tix[:, :, 0:2]).then_inc(S["lg_f"], 1)
            dve.wait_ge(S["lg_f"], 1)
            for t in range(TT):
                dve.tensor_scalar(wsel[:, t, :], iot[:, :], tixf[:, t, 0:1], 0.5, ALU.is_equal, ALU.mult)\
                    .then_inc(S["lg_eq"], 1)
                dve.tensor_scalar(wtmp[:, t, :], iot[:, :], tixf[:, t, 1:2], 0.5, ALU.is_equal, ALU.mult)\
                    .then_inc(S["lg_eq"], 1)
            dve.wait_ge(S["lg_eq"], 2 * TT)
            dve.tensor_tensor(wsel[:, :, :], wsel[:, :, :], wtmp[:, :, :], ALU.add).then_inc(S["lg_w"], 1)
            dve.wait_ge(S["ld_be"], 16)

            def bias(ep, u, t, first=False):
                J = 8 * ep + 4 * u + t
                dve.wait_ge(S["f_mm"], J + 1)
                if not (first and u == 0 and t < 2):
                    dve.wait_ge(S["relu_done"], J - 1)
                dve.tensor_tensor(zb[t % 2], fbank[t], be_s[:, 2 * ep + u, :], ALU.add).then_inc(S["z_done"], 1)

            def gather(J, t):
                dve.wait_ge(S["relu_done"], J + 1)
                dve.tensor_tensor(x1[:, t, :], x1[:, t, :], rb[t % 2], ALU.add).then_inc(S["acc_done"], 1)

            for u in range(2):
                for t in range(TT):
                    bias(0, u, t, first=True)
                    if u or t:
                        if 4 * u + t > 4:
                            dve.wait_ge(S["acc_done"], 4 * u + t - 4)
                        gather(4 * u + t - 1, (t - 1) % 4)
            def experts(ep, final=False):
                for u in range(2):
                    for t in range(TT):
                        bias(ep, u, t)
                        J = 8 * ep + 4 * u + t
                        dve.wait_ge(S["acc_done"], J - 4)
                        gather(J - 1, (t - 1) % 4)
                        if final and u == 1 and t == 2:
                            dve.wait_ge(S["acc_done"], J)
                            stats(4)
            with dve.Fori(1, NE // 2 - 1) as ep:
                experts(ep)
            experts(NE // 2 - 1, final=True)
            dve.wait_ge(S["acc_done"], 4 * NE - 1)
            stats(5, (0,), end=False)
            gather(4 * NE - 1, 3)
            dve.wait_ge(S["acc_done"], 4 * NE)
            stats(5, (1,))
            apply_norm(4)
            apply_norm(5)

        @block.tensor
        def _(pe):
            pe.wait_ge(S["ld_wx"], 16)
            for c in range(HC):
                pe.wait_ge(x_ld[c], 16)
                last = pe.matmul(PS[1][0:48, 512:1024], wx_s[:, c, :], xT_s[:, c, :], start=(c == 0), stop=(c == HC - 1))
            last.then_inc(S["xp_mm"], 1)
            pe.wait_ge(S["xp_sb"], 1)
            pe.wait_ge(S["ld_small"], 16 * N_SMALL)
            for b in range(NB):
                for c in range(HC):
                    pe.matmul(dtp[b][c], wdt_s[0:DTR, c * P:(c + 1) * P], xp_s[0:DTR, b * SX:(b + 1) * SX],
                              start=True, stop=True).then_inc(S["dtl_mm"], 1)
            pe.wait_ge(S["const_ready"], 2)

            PASS = ((0, 0), (0, 1), (1, 0))

            def kv_block(j, blk, src, w0):
                if blk < 2:
                    pe.wait_ge(S["k_n"], 2 * j + blk + 1)
                else:
                    pe.wait_ge(S["v_lo"], 2 * j + blk - 1)
                m = 0
                for a, w in PASS:
                    for c in range(HC):
                        last = pe.matmul(kvp[blk], src(a, c), pc[w][:, w0 + c, :], start=(m == 0), stop=(m == 11))
                        m += 1
                last.then_inc(S["kv_mm"], 1)

            def k_transpose(j, blk):
                pe.wait_ge(S["k_n"], 2 * j + blk + 3)
                pe.wait_ge(S["k_lo"], 2 * j + blk + 1)
                for h in range(4):
                    last = pe.transpose(ktp[blk][:, h * P:(h + 1) * P], kn[blk][:, h * P:(h + 1) * P], ident[:, :])
                last.then_inc(S["k_tr"], 1)

            def y_sum(b, i, pair):
                j = i + HC * b
                if pair == 0:
                    pe.wait_ge(S["xd_ready"], j + 1)
                    pe.wait_ge(S["r_ev"], j + 1)
                    for t in range(2):
                        pe.matmul(yp[:, t, :], xd[:, t * P:(t + 1) * P], ident[:, :], start=True, stop=False)
                pe.wait_ge(S["pair_added_v"] if pair else S["pair_added_p"], j + 1)
                for t in range(2):
                    for n in range(NPC):
                        at = n * SX + t * P
                        last = pe.matmul(yp[:, t, :], W[2 * pair + 1][:, at:at + P], ident[:, :], start=False,
                                         stop=(pair == 1 and n == NPC - 1))
                last.then_inc(S["y_mm"], 1)

            pe.sem_inc(S["v_lo"], 2)
            pe.sem_inc(S["k_lo"], 2)
            pe.sem_inc(S["k_tr"], 2)
            pe.sem_inc(S["k_n"], 2)
            pe.sem_inc(S["y_mm"], 2)
            pe.sem_inc(S["r_ev"], 1)
            for b in range(NB):
                with pe.Fori(0, HC) as i:
                    j = i + HC * b

                    def src(a, c):
                        return pc[a][:, PC_C[b] + j, c * P:(c + 1) * P]

                    def splits(groups):
                        pe.wait_ge(S["split_v"], 2 * groups)
                        pe.wait_ge(S["split_p"], 2 * groups)
                    splits((3, 6)[b])
                    kv_block(j, 0, src, PC_K)
                    kv_block(j, 1, src, PC_K + 4)
                    splits((4, 6)[b])
                    kv_block(j, 2, src, PC_V)
                    splits((5, 6)[b])
                    pe.wait_ge(S["sp_max"], 2 * HC)
                    kv_block(j, 3, src, PC_V + 4)
                    y_sum(b, i, 0)
                    y_sum(b, i, 1)
                    k_transpose(j, 0)
                    k_transpose(j, 1)

            def xT_transpose(m):
                pe.wait_ge(S["ln_x"], 2 * m + 2)
                for c in range(HC):
                    for t in range(2):
                        last = pe.transpose(xtb[m][c // 2][:, c % 2 * SX + t * P:c % 2 * SX + (t + 1) * P],
                                            x1[:, m % 2 * 2 + t, c * P:(c + 1) * P], ident[:, :])
                    if c % 2:
                        last.then_inc(S["xT_tr"], 1)

            def kv_products(t, between=None):
                def src(a, c):
                    return xh[a][:, c, bass.ts(t, P)]
                j = t + CT
                kv_block(j, 0, src, PC_K)
                kv_block(j, 1, src, PC_K + 4)
                if between:
                    between()
                kv_block(j, 2, src, PC_V)
                kv_block(j, 3, src, PC_V + 4)

            def kv_transposes(t):
                k_transpose(t + CT, 0)
                k_transpose(t + CT, 1)

            pe.wait_ge(S["k_n"], 2 * CT + 2)
            xT_transpose(0)
            pe.wait_ge(S["xT_lo"], 2)
            pe.wait_ge(S["r_ev"], NB * HC + 1)
            kv_products(0, between=lambda: xT_transpose(1))
            kv_transposes(0)
            pe.wait_ge(S["xT_lo"], 4)
            with pe.Fori(1, TT - 1) as t:
                kv_products(t)
                kv_transposes(t)

            def q_job(g, h, bank=PG):
                if h == 0:
                    pe.wait_ge(S["a_split"], g + 1)
                m = 0
                for w, a in PASS:
                    for c in range(HC):
                        last = pe.matmul(bank[:, :], wA[w][:, c, h * HD:(h + 1) * HD], xh[a][:, c, :],
                                         start=(m == 0), stop=(m == 11))
                        m += 1
                last.then_inc(S["q_mm"], 1)

            def ss_job(g, h, bank=PG):
                pe.wait_ge(S["q_sq"], 4 * g + h + 1)
                pe.wait_ge(S["q_lo"], 4 * g + h + 1)
                for t in range(TT):
                    last = pe.matmul(bank[:, t:t + 1], sqq[:, t * P:(t + 1) * P], ones[:, :], start=True, stop=True)
                last.then_inc(S["ss_mm"], 1)

            def wo_job(g, t, bank=PG, heads=range(GRP)):
                for h in heads:
                    if t == 0 and h == 0:
                        pe.wait_ge(S["b_split"], g + 1)
                        pe.wait_ge(S["o_lo"], 4 * g + 3)
                    if t == 0 and h == GRP - 1:
                        pe.wait_ge(S["o_lo"], 4 * g + 4)
                    for a, w in PASS:
                        last = pe.matmul(bank[:, :], oT[a][:, h, t * P:(t + 1) * P], wB[w][:, h, :],
                                         start=(h == 0 and (a, w) == PASS[0]),
                                         stop=(h == GRP - 1 and (a, w) == PASS[-1]))
                if GRP - 1 in heads:
                    last.then_inc(S["wo_mm"], 1)

            def scores(g, s, n, first):
                h, t = s // 4, s % 4
                b = t // 2
                if not (first and s < 2):
                    pe.wait_ge(S["exp_done"], n - 1)
                if t == 0:
                    pe.wait_ge(S["q_lo"], 4 * g + h + 1)
                for m, (a, w) in enumerate(PASS):
                    pe.matmul(PS[s % 2][:, 0:SC], q[a][:, h, t * P:(t + 1) * P], kTc[w][:, g, b * SC:(b + 1) * SC],
                              start=(m == 0), stop=(m == 2))
                for m, (a, w) in enumerate(PASS):
                    last = pe.matmul(PS[s % 2][:, SC:KL], q[a][:, h, t * P:(t + 1) * P],
                                     kTx[w][:, g, b * KX:(b + 1) * KX], start=(m == 0), stop=(m == 2))
                last.then_inc(S["s_mm"], 1)

            def probs_T(s, n, first):
                pe.wait_ge(S["norm_done"], n - 1)
                for k in range(KT):
                    if k in (0, 4) and not (first and s < 3):
                        pe.wait_ge(S["pt_lo" if k else "pt_lo1"], n - 2)
                    last = pe.transpose(PTT[:, k * P:(k + 1) * P], Pb[(s - 2) % 4][:, k * P:(k + 1) * P], ident[:, :])
                last.then_inc(S["t_done"], 1)

            def values(g, s, n, first, after_half=False):
                k4 = (s - 3) % SLOTS
                t = k4 % 4
                b = t // 2
                pe.wait_ge(S["pt_lo"], n - 2)
                if t == 0 and not (first and s == 3):
                    pe.wait_ge(S["o_lo"], 4 * g + k4 // 4)
                if after_half:
                    pe.wait_ge(S["o_lo"], 4 * KVH)
                m = 0
                for w, a in PASS:
                    for k in range(KT):
                        v = Vc[w][:, b * 4 + k, bass.ts(g, HD)] if k < 4 else Vx[w][:, b * 2 + k - 4, bass.ts(g, HD)]
                        last = pe.matmul(PO[:, t * P:(t + 1) * P], v, pt[(s - 3) % 2][a][:, k, :],
                                         start=(m == 0), stop=(m == 3 * KT - 1))
                        m += 1
                last.then_inc(S["pv_done"], 1)

            def slot(g, s, first=False, final=False):
                n = SLOTS * g + s
                scores(g, s, n, first)
                if not (first and s < 2):
                    probs_T(s, n, first)
                if s % 4 != 3 and not (first and s < 3):
                    values(g if s >= 3 else g - 1, s, n, first)
                if s in SS_AT[2:]:
                    if s == SS_AT[3] and not first:
                        pe.wait_ge(S["wo_add"], 4 * g)
                    ss_job(g, SS_AT.index(s))
                if s in WO_AT and not first:
                    t = WO_AT.index(s)
                    if t == 0:
                        pe.wait_ge(S["q_lo"], 4 * g + 4)
                    else:
                        pe.wait_ge(S["wo_add"], 4 * g - 4 + t)
                    wo_job(g - 1, t)
                if s == Q_AT[3]:
                    pe.wait_ge(S["ss_read"], 4 * g + 3)
                    q_job(g, 3)
                if not final:
                    if s in Q_AT[:3]:
                        h = Q_AT.index(s)
                        pe.wait_ge(S["ss_read"], 4 * g + 4 + h)
                        q_job(g + 1, h)
                    if s in SS_AT[:2]:
                        ss_job(g + 1, SS_AT.index(s))
                if s % 4 == 3:
                    values(g, s, n, first)

            kv_products(TT - 1)
            q_job(0, 0, q0b[0])
            kv_transposes(TT - 1)
            q_job(0, 1, q0b[1])
            ss_job(0, 0, q0b[0])
            pe.wait_ge(S["v_lo"], 2 * (CT + TT) + 2)
            q_job(0, 2, q0b[2])
            ss_job(0, 1, q0b[1])
            pe.wait_ge(S["k_lo"], 2 * (CT + TT) + 2)
            for s in range(SLOTS):
                slot(0, s, first=True)
            with pe.Fori(1, KVH - 1) as g:
                for s in range(SLOTS):
                    slot(g, s)
            for s in range(SLOTS):
                slot(KVH - 1, s, final=True)
            n = SLOTS * KVH
            probs_T(0, n, False)
            values(KVH - 1, 0, n, False)
            pe.wait_ge(S["exp_done"], n - 1)
            for heads in (range(GRP - 1), (GRP - 1,)):
                for t in (0, 1):
                    wo_job(KVH - 1, t, fbank[t], heads)
            probs_T(1, n + 1, False)
            values(KVH - 1, 1, n + 1, False, after_half=True)
            pe.wait_ge(S["exp_done"], n)
            wo_job(KVH - 1, 2, fbank[2], range(GRP - 1))
            values(KVH - 1, 2, n + 2, False)
            xT_transpose(2)
            wo_job(KVH - 1, 3, fbank[3], range(GRP - 1))
            pe.wait_ge(S["o_lo"], 4 * KVH + 1)
            for t in (2, 3):
                wo_job(KVH - 1, t, fbank[t], (GRP - 1,))

            def logits(b):
                pe.wait_ge(S["xT_f"], 2 * b + 2)
                for t in (2 * b, 2 * b + 1):
                    for c in range(HC):
                        last = pe.matmul(PTT[:, t * NE:(t + 1) * NE], x2T[:, c, t * P:(t + 1) * P], wg_s[:, c, :],
                                         start=(c == 0), stop=(c == HC - 1))
                    last.then_inc(S["lg_mm"], 1)

            def expert(ep, u, first=False):
                pe.wait_ge(S[("a_split", "b_split")[u]], KVH + 1 + ep)
                w = (wA, wB)[u]
                for t in range(TT):
                    if first and u == 0:
                        if t == 2:
                            xT_transpose(3)
                            logits(0)
                        if t == 3:
                            logits(1)
                        pe.wait_ge(S["wo_add"], 4 * (KVH - 1) + t + 1)
                        pe.wait_ge(S["xT_lo"], 6 + t // 2 * 2)
                    else:
                        pe.wait_ge(S["z_done"], 8 * ep + 4 * u + t - 3)
                    m = 0
                    for a, l in PASS:
                        for c in range(HC):
                            last = pe.matmul(fbank[t], xh[a][:, c, t * P:(t + 1) * P], w[l][:, c, :],
                                             start=(m == 0), stop=(m == 11))
                            m += 1
                    last.then_inc(S["f_mm"], 1)
            expert(0, 0, first=True)
            expert(0, 1)
            with pe.Fori(1, NE // 2) as ep:
                expert(ep, 0)
                expert(ep, 1)


def flat(a):
    return a.rearrange("p c t -> p (c t)")


def kernel(x, ctx_4096, L0_attn_A_log, L0_attn_D, L0_attn_x_proj_w, L0_attn_dt_proj_w, L0_attn_dt_proj_b,
           L0_xattn_Wq, L0_xattn_Wk, L0_xattn_Wv, L0_xattn_Wo, L0_xattn_q_norm_w, L0_xattn_k_norm_w,
           L0_ffn_W_gate, L0_ffn_b_gate, L0_ffn_W_e, L0_ffn_b_e):
    import numpy as np
    import concourse.bacc as bacc
    from concourse.bass_utils import run_bass_kernel_spmd

    def a(v):
        return np.asarray(v)

    def chunked(w, cols):
        w = a(w)
        return w.reshape(HC, P, -1, cols).transpose(2, 1, 0, 3)

    wk, wv = chunked(L0_xattn_Wk, DM), chunked(L0_xattn_Wv, DM)
    ctx_t = a(ctx_4096).reshape(CT, P, HC, P).transpose(0, 3, 2, 1)
    ctx_t = ctx_t.reshape(CT, P, DM)
    pieces = np.concatenate([wk.transpose(0, 2, 1, 3).reshape(8, P, DM), ctx_t[:CT // 2],
                             wv.transpose(0, 2, 1, 3).reshape(8, P, DM), ctx_t[CT // 2:]])
    wq = chunked(L0_xattn_Wq, GRP * HD)
    wo = a(L0_xattn_Wo).reshape(KVH, GRP, HD, DM).transpose(0, 2, 1, 3)
    we = a(L0_ffn_W_e).reshape(NE, HC, P, DM).transpose(0, 2, 1, 3)
    arrays = {
        "xT": a(x).reshape(NT, DM).T,
        "pieces": pieces,
        "wx": a(L0_attn_x_proj_w).T,
        "wdt": a(L0_attn_dt_proj_w).T,
        "dtb": a(L0_attn_dt_proj_b).reshape(HC, P).T,
        "alog": a(L0_attn_A_log).reshape(HC, P, NS).transpose(1, 0, 2).reshape(P, HC * NS),
        "dskip": a(L0_attn_D).reshape(HC, P).T,
        "qnw": a(L0_xattn_q_norm_w).reshape(HD, 1),
        "knw": a(L0_xattn_k_norm_w).reshape(HD, 1),
        "wa": np.concatenate([wq, we[0::2]]),
        "wb": np.concatenate([wo, we[1::2]]),
        "wg": a(L0_ffn_W_gate),
        "bg": a(L0_ffn_b_gate),
        "be": a(L0_ffn_b_e),
    }
    nc = bacc.Bacc("TRN2", target_bir_lowering=False, num_devices=1)
    arrays = {k: np.ascontiguousarray(v) for k, v in arrays.items()}
    args = {k: nc.dram_tensor(k, v.shape, mybir.dt.from_np(v.dtype), kind="ExternalInput").ap() for k, v in arrays.items()}
    args["scratch"] = nc.dram_tensor("scratch", (2 * NS, NT), fp32).ap()
    args["out"] = nc.dram_tensor("out", (TT, P, DM), fp32, kind="ExternalOutput").ap()
    decoder_layer(nc, **args)
    r = run_bass_kernel_spmd(nc, [arrays], core_ids=[0])
    return np.asarray(r.results[0]["out"]).reshape(NB, SX, DM)
```
